# Optimizing a Trainium2 kernel written in Bass

```python
import numpy as np
import jax
import jax.numpy as jnp

def _softmax(x, axis=-1):
    return jax.nn.softmax(x, axis=axis)

def _gelu(x):
    return jax.nn.gelu(x, approximate=True)

def _silu(x):
    return jax.nn.silu(x)

def _sigmoid(x):
    return jax.nn.sigmoid(x)

def _layernorm(x, axis=-1, eps=1e-05):
    m = jnp.mean(x, axis=axis, keepdims=True)
    v = jnp.var(x, axis=axis, keepdims=True)
    return (x - m) / jnp.sqrt(v + eps)

def _scatter_add(tgt, idx, src, axis=0):
    return tgt.at[idx].add(src)

def _segment_sum(src, seg, n):
    return jax.ops.segment_sum(src, seg, n)
kernel_name = 'mk_xattn_ffn_d1_seqx_r8_67b0f0'

def setup_inputs(seed: int=0):
    np.random.seed(seed)
    _w = jnp.asarray

    def _rec_inputs():
        import jax
        import jax.numpy as jnp
        _rk = jax.random.key(seed)
        x = -0.0002928 + 1 * jax.random.normal(jax.random.fold_in(_rk, 1), (64, 64, 256), jnp.float32)
        _lenS = 64 - jax.random.randint(jax.random.fold_in(_rk, 7), (64,), 0, max(1, 64 // 4) + 1, jnp.int32)
        _lenS2 = 64 - jax.random.randint(jax.random.fold_in(_rk, 8), (64,), 0, max(1, 64 // 4) + 1, jnp.int32)
        _ctx_2048P = jax.random.normal(jax.random.fold_in(_rk, 11), (64, 16, 256), jnp.float32)
        _ctx_2048c = jax.random.dirichlet(jax.random.fold_in(_rk, 511), 0.3 * jnp.ones((16,), jnp.float32), (64, 64))
        _ctx_2048t = jnp.einsum('bsk,bkd->bsd', _ctx_2048c, _ctx_2048P)
        _ctx_2048t = _ctx_2048t * jax.lax.rsqrt(jnp.mean(jnp.square(_ctx_2048t)) + 1e-12) * 0.953939
        ctx_2048 = -1.39393e-06 + 0.999914 * (_ctx_2048t + 0.3 * jax.random.normal(jax.random.fold_in(_rk, 611), (64, 64, 256), jnp.float32))
        return (x, ctx_2048)
    x, ctx_2048 = _rec_inputs()

    def _L0_xattn_setup():
        import jax, jax.numpy as jnp
        import numpy as np
        HEADS = 8
        DIM_HEAD = 64
        HIDDEN = HEADS * DIM_HEAD
        key = jax.random.key(seed)
        ks = jax.random.split(key, 5)
        b, dim, n = (4, 64, 256)
        ctx_dim, m = (64, 256)
        x = jax.random.normal(ks[0], (b, dim, n), dtype=jnp.float32)
        context = jax.random.normal(ks[1], (b, ctx_dim, m), dtype=jnp.float32)
        Wq = jax.random.normal(ks[2], (HIDDEN, dim), dtype=jnp.float32) / np.sqrt(dim).astype(np.float32)
        Wkv = jax.random.normal(ks[3], (2 * HIDDEN, ctx_dim), dtype=jnp.float32) / np.sqrt(ctx_dim).astype(np.float32)
        Wout = jax.random.normal(ks[4], (dim, HIDDEN), dtype=jnp.float32) / np.sqrt(HIDDEN).astype(np.float32)
        bout = jnp.zeros((dim,), dtype=jnp.float32)
        return {'x': x, 'context': context, 'Wq': Wq, 'Wkv': Wkv, 'Wout': Wout, 'bout': bout}
    _L0_xattn_all = _L0_xattn_setup()
    _L0_xattn_in = {k: v for k, v in _L0_xattn_all.items() if k in ('Wq', 'Wkv', 'Wout', 'bout')}
    del _L0_xattn_all

    def _L0_ffn_setup():
        import jax, jax.numpy as jnp
        import numpy as np
        HIDDEN = 256
        INTER = 704
        B, S = (2, 256)

        def _ternary(key, shape):
            return jax.random.randint(key, shape, -1, 2).astype(jnp.float32)
        key = jax.random.key(seed)
        ks = jax.random.split(key, 7)
        x = jax.random.normal(ks[0], (B, S, HIDDEN), dtype=jnp.float32)
        gate_w = _ternary(ks[1], (INTER, HIDDEN))
        up_w = _ternary(ks[2], (INTER, HIDDEN))
        down_w = _ternary(ks[3], (HIDDEN, INTER))
        gate_s = jax.random.uniform(ks[4], (INTER,), minval=0.01, maxval=0.1, dtype=jnp.float32)
        up_s = jax.random.uniform(ks[5], (INTER,), minval=0.01, maxval=0.1, dtype=jnp.float32)
        down_s = jax.random.uniform(ks[6], (HIDDEN,), minval=0.01, maxval=0.1, dtype=jnp.float32)
        return {'x': x, 'gate_w': gate_w, 'up_w': up_w, 'down_w': down_w, 'gate_s': gate_s, 'up_s': up_s, 'down_s': down_s}
    _L0_ffn_all = _L0_ffn_setup()
    _L0_ffn_in = {k: v for k, v in _L0_ffn_all.items() if k in ('gate_w', 'up_w', 'down_w', 'gate_s', 'up_s', 'down_s')}
    del _L0_ffn_all
    return {'x': x, 'ctx_2048': ctx_2048, 'L0_xattn_Wq': _L0_xattn_in['Wq'], 'L0_xattn_Wkv': _L0_xattn_in['Wkv'], 'L0_xattn_Wout': _L0_xattn_in['Wout'], 'L0_xattn_bout': _L0_xattn_in['bout'], 'L0_ffn_gate_w': _L0_ffn_in['gate_w'], 'L0_ffn_up_w': _L0_ffn_in['up_w'], 'L0_ffn_down_w': _L0_ffn_in['down_w'], 'L0_ffn_gate_s': _L0_ffn_in['gate_s'], 'L0_ffn_up_s': _L0_ffn_in['up_s'], 'L0_ffn_down_s': _L0_ffn_in['down_s']}

def reference(x, ctx_2048, L0_xattn_Wq, L0_xattn_Wkv, L0_xattn_Wout, L0_xattn_bout, L0_ffn_gate_w, L0_ffn_up_w, L0_ffn_down_w, L0_ffn_gate_s, L0_ffn_up_s, L0_ffn_down_s):
    import jax
    import jax.numpy as jnp

    def _L0_xattn_ref(x, context, Wq, Wkv, Wout, bout):
        import jax, jax.numpy as jnp
        import numpy as np
        HEADS = 8
        DIM_HEAD = 64
        HIDDEN = HEADS * DIM_HEAD
        b = x.shape[0]
        q = jnp.einsum('oc,bcn->bon', Wq, x)
        kv = jnp.einsum('oc,bcm->bom', Wkv, context)
        k, v = jnp.split(kv, 2, axis=1)
        split_heads = lambda t: t.reshape(b, HEADS, DIM_HEAD, t.shape[-1])
        q, k, v = (split_heads(q), split_heads(k), split_heads(v))
        sim = jnp.einsum('bhdi,bhdj->bhij', q, k)
        attn = jax.nn.softmax(sim, axis=-1)
        out = jnp.einsum('bhij,bhdj->bhid', attn, v)
        out = jnp.transpose(out, (0, 1, 3, 2)).reshape(b, HIDDEN, -1)
        return jnp.einsum('oc,bcn->bon', Wout, out) + bout[None, :, None]

    def _L0_ffn_ref(x, gate_w, up_w, down_w, gate_s, up_s, down_s):
        import jax, jax.numpy as jnp
        import numpy as np
        HIDDEN = 256
        INTER = 704
        B, S = (2, 256)

        def _ternary(key, shape):
            return jax.random.randint(key, shape, -1, 2).astype(jnp.float32)
        b, s, h = x.shape
        xf = x.reshape(b * s, h)
        g = jnp.einsum('th,ih->ti', xf, gate_w) * gate_s
        u = jnp.einsum('th,ih->ti', xf, up_w) * up_s
        hdn = jax.nn.silu(g) * u
        out = jnp.einsum('ti,hi->th', hdn, down_w) * down_s
        return out.reshape(b, s, -1)
    x = x + _L0_xattn_ref(_layernorm(x, axis=-1), ctx_2048, L0_xattn_Wq, L0_xattn_Wkv, L0_xattn_Wout, L0_xattn_bout)
    x = x + _L0_ffn_ref(_layernorm(x, axis=-1), L0_ffn_gate_w, L0_ffn_up_w, L0_ffn_down_w, L0_ffn_gate_s, L0_ffn_up_s, L0_ffn_down_s)
    return x

_drawn_inputs = setup_inputs


def setup_inputs(seed=0):
    import zlib

    import numpy as np

    out = dict(_drawn_inputs(seed))
    spreads = {'L0_xattn_bout': (0.0, 0.1)}
    factors = {}
    for name, (base, spread) in spreads.items():
        noise = np.random.default_rng([zlib.crc32(name.encode()), seed]).standard_normal(out[name].shape)
        drawn = base * np.exp(spread * noise) if base else spread * noise
        out[name] = jnp.asarray(drawn.astype(out[name].dtype))
    for name, factor in factors.items():
        out[name] = (out[name] * factor).astype(out[name].dtype)
    return out
```

```python
from contextlib import ExitStack

import concourse.bass as bass
from concourse import mybir

ALU = mybir.AluOpType
ACT = mybir.ActivationFunctionType
F32 = mybir.dt.float32
F16 = mybir.dt.float16
AX_X = mybir.AxisListType.X

P = 128
EPS = 1e-5
SC = 16.0
BODY = 4
RING = 4
LAG_PROJ, LAG_MAX, LAG_ATT, LAG_SUM, LAG_FFN = 1, 2, 3, 4, 6


class At:

    def __init__(self, g, per, off, total):
        self.g, self.per, self.off, self.total = g, per, off, total

    def live(self):
        return not isinstance(self.g, int) or 0 <= self.per * self.g + self.off < self.total

    def back(self, k):
        return At(self.g, self.per, self.off - k, self.total)

    def done(self, n, k):
        return self.g * (self.per * n) + (self.off * n + k)

    def landed(self, slots, inc):
        if isinstance(self.g, int):
            return ((self.per * self.g + self.off) // slots + 1) * inc
        return self.g * (self.per // slots * inc) + (self.off // slots + 1) * inc


def wait(eng, sem, value):
    if not isinstance(value, int) or value > 0:
        eng.wait_ge(sem, value)


def xattn_ffn(nc, x, ctx_in, wq, wkv, wout, bout, gate_w, up_w, down_w, gate_s, up_s, down_s, out):
    NB, C, N = x.shape
    HID = wq.shape[0]
    D = 64
    H = HID // D
    INTER = gate_w.shape[0]
    NPAIR = NB // 2
    IT = N // P
    FT = INTER // P
    TAIL = INTER - FT * P
    assert C == D == 64 and N == 256 and H == 8 and FT == 5 and TAIL == 64
    HC = H * D
    GW = D + 1
    HG = H // 2
    ROUNDS = [["g0", "g1", "u0", "u1"], ["g2", "g3", "u2", "u3"], ["g4", "t", "u4"]]
    TILES = [name for r in ROUNDS for name in r]

    with ExitStack() as stack:
        def sb(name, shape, dt=F32):
            return stack.enter_context(nc.sbuf_tensor(name, shape, dt))

        def psum(name, shape):
            return stack.enter_context(nc.psum_tensor(name, shape, F32))

        def sem(name):
            return stack.enter_context(nc.semaphore(name))

        ident = sb("ident", [P, P])
        neg_half = sb("neg_half", [P, 1])
        wq_sb = sb("wq_sb", [D, H, D])
        wk2 = sb("wk2", [D, H, 2, D])
        wv2 = sb("wv2", [D, H, 2, D])
        wout_sb = sb("wout_sb", [D, HC])
        woutT = sb("woutT", [D, HC])
        gate_raw = sb("gate_raw", [P, FT + 1, N])
        up_raw = sb("up_raw", [P, FT + 1, N])
        down_raw = sb("down_raw", [P, 2, INTER])
        tail_raw = sb("tail_raw", [P, N])
        gs_col = sb("gs_col", [P, FT + 1])
        us_col = sb("us_col", [P, FT + 1])
        ts_col = sb("ts_col", [P, 1])
        ds_col = sb("ds_col", [P, 2])
        bout_col = sb("bout_col", [P, 1])
        a_w = sb("a_w", [P, HC], F16)
        b_w = sb("b_w", [P, HC], F16)
        gu_hi = sb("gu_hi", [P, 2, len(TILES), P], F16)
        gu_lo = sb("gu_lo", [P, 2, len(TILES), P], F16)
        dn_hi = sb("dn_hi", [P, FT + 1, N], F16)
        dn_lo = sb("dn_lo", [P, FT + 1, N], F16)
        x_in = sb("x_in", [P, 4, N])
        c_in = sb("c_in", [P, 4, N])
        c_hi = sb("c_hi", [P, 2, N], F16)
        c_lo = sb("c_lo", [P, 2, N], F16)
        stats = sb("stats", [P, 2, 6])
        mv = sb("mv", [P, 2, 2])
        var = sb("var", [P, 2, 1])
        rstd = sb("rstd", [P, 2, 1])
        xn = sb("xn", [P, 2, N])
        x_hi = sb("x_hi", [P, 4, N], F16)
        x_lom = sb("x_lom", [P, 4, N], F16)
        k_hl = sb("k_hl", [P, 4, H, N], F16)
        k_hm = sb("k_hm", [P, 4, H, N], F16)
        g_hi = sb("g_hi", [P, 4, IT, H, GW], F16)
        g_lo = sb("g_lo", [P, 4, IT, H, D], F16)
        nmax = sb("nmax", [P, 2, IT, H])
        p_f = sb("p_f", [P, 2, HG, N])
        p_hi = sb("p_hi", [P, 4, HG, N], F16)
        p_lo = sb("p_lo", [P, 4, HG, N], F16)
        rsum = sb("rsum", [P, 4, HG, 1])
        heads = sb("heads", [P, 2, H, IT, D])
        half = sb("half", [P, 4, IT, D])
        quar = sb("quar", [P, 2, IT, D])
        yT = sb("yT", [P, 2, IT, 2, D])
        x_pair = sb("x_pair", [P, 2, N])
        x2 = sb("x2", [P, 2, N])
        stats2 = sb("stats2", [P, 6])
        mv2 = sb("mv2", [P, 2])
        var2 = sb("var2", [P, 1])
        rstd2 = sb("rstd2", [P, 1])
        xn2 = sb("xn2", [P, N])
        xt_hi = sb("xt_hi", [P, 2, P], F16)
        xt_lo = sb("xt_lo", [P, 2, P], F16)
        th = sb("th", [P, 2, 2, P])
        tg = sb("tg", [P, 2, 2, P])
        h_f = sb("h_f", [P, 2, 2, P])
        h_hi = sb("h_hi", [P, FT + 1, P], F16)
        h_lo = sb("h_lo", [P, FT + 1, P], F16)
        y_out = sb("y_out", [P, 2, N])

        s_bank = [psum(f"s_bank{i}", [P, 2, 512]) for i in range(2)]
        ring = [psum(f"ring{i}", [P, 512]) for i in range(RING)]

        ld_w, ld_f = sem("ld_w"), sem("ld_f")
        ld_x = [sem(f"ld_x{i}") for i in range(4)]
        ld_c = [sem(f"ld_c{i}") for i in range(4)]
        ld_p = [sem(f"ld_p{i}") for i in range(2)]
        st_y = [sem(f"st_y{i}") for i in range(2)]
        memset_done, const_done, half_done = sem("memset_done"), sem("const_done"), sem("half_done")
        setup_mm, setup_ev = sem("setup_mm"), sem("setup_ev")
        tail_scaled = sem("tail_scaled")
        weights_ready = sem("weights_ready")
        k_mm, g_mm, mx_mm, mt_mm, s_mm, av_mm = map(sem, ("k_mm", "g_mm", "mx_mm", "mt_mm", "s_mm", "av_mm"))
        yt_mm, xt_mm, r_mm, d_mm = map(sem, ("yt_mm", "xt_mm", "r_mm", "d_mm"))
        st_done, ag_done, va_done, xn_done = map(sem, ("st_done", "ag_done", "va_done", "xn_done"))
        mx_done, rs_done, av_done = map(sem, ("mx_done", "rs_done", "av_done"))
        klo_done, km_done, glo_done = map(sem, ("klo_done", "km_done", "glo_done"))
        x2_done, st2_done, ag2_done, va2_done, xn2_done, xtlo_done, tg_done, h_done, y_done = map(
            sem, ("x2_done", "st2_done", "ag2_done", "va2_done", "xn2_done", "xtlo_done", "tg_done", "h_done",
                  "y_done"))
        chi_done, xhi_done, mrow_done, khi_done, ghi_done, exp_done, phi_done = map(
            sem, ("chi_done", "xhi_done", "mrow_done", "khi_done", "ghi_done", "exp_done", "phi_done"))
        xthi_done, th_done, hhi_done = map(sem, ("xthi_done", "th_done", "hhi_done"))
        rstd_done, clo_done, xlo_done, plo_done, ad1_done, ad2_done, ad3_done = map(
            sem, ("rstd_done", "clo_done", "xlo_done", "plo_done", "ad1_done", "ad2_done", "ad3_done"))
        rstd2_done, hlo_done = sem("rstd2_done"), sem("hlo_done")

        def stages(g, t):
            entry = lambda lag: At(g, BODY, t - lag, NB)
            pair = At(g, 2, (t - LAG_FFN) // 2, NPAIR)
            return entry(0), entry(LAG_PROJ), entry(LAG_MAX), entry(LAG_ATT), entry(LAG_SUM), pair

        def uses(g, t):
            _, e1, e2, e3, e4, pr = stages(g, t)
            even = t % 2 == 0
            first = [("mx", e2, 0), ("mx", e2, 1), ("mx", e2, 2), ("av", e4, 1), ("k", e1, 0)]
            second = [("mx", e2, 3), ("mx", e2, 4), ("mx", e2, 5), ("av", e4, 2), ("k", e1, 1)]
            third = [("mx", e2, 6), ("mx", e2, 7), ("av", e4, 3), ("g", e1, 0)]
            fourth = [("av", e3, 0), ("g", e1, 1), ("mt", e2, 0)]
            if even:
                return [first + [("yt", pr, 0)], second, third + [("xt", pr, 0)], fourth + [("r", pr, 0)]]
            return [first + [("r", pr, 1)], second + [("r", pr, 2)], third, fourth + [("d", pr, 0)]]

        READ = {
            "mx": (mx_done, 8, lambda k: k + 1), "av": (av_done, 4, lambda k: k + 1),
            "k": (klo_done, 4, lambda k: 2 * k + 2), "g": (glo_done, 2, lambda k: k + 1),
            "mt": (mrow_done, 1, lambda k: 1), "yt": (x2_done, 1, lambda k: 1),
            "xt": (xtlo_done, 1, lambda k: 1), "r": (h_done, 3, lambda k: k + 1), "d": (y_done, 1, lambda k: 1),
        }
        ORDER = [[u for quarter in uses(0, t) for u in quarter] for t in (0, 1)]
        assert (len(ORDER[0]) + len(ORDER[1])) % RING == 0

        def position(t, kind, k):
            names = [(u[0], u[2]) for u in ORDER[t % 2]]
            return (len(ORDER[0]) if t % 2 else 0) + names.index((kind, k))

        def bank(t, kind, k):
            return ring[position(t, kind, k) % RING]

        def bank_free(pe, g, t, kind, k):
            back = 0
            place = position(t, kind, k)
            while True:
                back += RING
                at, tt, gg = place - back, t - t % 2, g
                while at < 0:
                    at += len(ORDER[0]) + len(ORDER[1])
                    tt -= 2
                if isinstance(g, int):
                    if 4 * g + tt < 0:
                        return
                tt += 1 if at >= len(ORDER[0]) else 0
                at -= len(ORDER[0]) if at >= len(ORDER[0]) else 0
                if tt < 0 and isinstance(g, int):
                    gg, tt = g - 1, tt + 4
                flat = [u for quarter in uses(gg, tt) for u in quarter]
                name, entry, n = flat[at]
                if entry.live():
                    read, per, last = READ[name]
                    wait(pe, read, entry.done(per, last(n)))
                    return

        block = stack.enter_context(nc.Block())

        GROUPS = (NB + LAG_FFN + 2 + BODY - 1) // BODY
        FIRST_FULL = 2
        LAST_FULL = NB // BODY

        def walk(eng, step, last_full=NB // BODY):
            for g in range(FIRST_FULL):
                for t in range(BODY):
                    step(g, t)
            with eng.Fori(FIRST_FULL, last_full) as g:
                for t in range(BODY):
                    step(g, t)
            for g in range(last_full, GROUPS):
                for t in range(BODY):
                    step(g, t)

        @block.sync
        def _(sp):
            kv = wkv.rearrange("(s h d) c -> s d h c", s=2, d=D)
            for c in range(2):
                sp.dma_start(wk2[:, :, c, :], kv[0]).then_inc(ld_w, 16)
                sp.dma_start(wv2[:, :, c, :], kv[1]).then_inc(ld_w, 16)
            sp.dma_start(wq_sb[:], wq.rearrange("(h d) c -> d h c", d=D)).then_inc(ld_w, 16)
            sp.dma_start(wout_sb[:], wout).then_inc(ld_w, 16)

            def load(e):
                if not e.live():
                    return
                slot = e.off % 4
                src_x, src_c = (v[bass.ds(e.g * BODY + e.off, 1)].rearrange("b c n -> (b c) n") for v in (x, ctx_in))
                wait(sp, xn_done, e.back(4).done(1, 1))
                for lo in (0, D):
                    sp.dma_start(x_in[lo:lo + D, slot, :], src_x).then_inc(ld_x[slot], 16)
                wait(sp, clo_done, e.back(4).done(1, 1))
                for lo in (0, D):
                    sp.dma_start(c_in[lo:lo + D, slot, :], src_c).then_inc(ld_c[slot], 16)

            def step(g, t):
                entry, pair = At(g, BODY, t + 3, NB), At(g, 2, (t - LAG_FFN) // 2, NPAIR)
                load(entry)
                if t % 2 == 0:
                    nxt = At(g, 2, (t - LAG_SUM) // 2, NPAIR)
                    if nxt.live():
                        slot = nxt.off % 2
                        wait(sp, x2_done, nxt.back(2).done(1, 1))
                        sp.dma_start(x_pair[:, slot, :], x[bass.ds(nxt.g * BODY + 2 * nxt.off, 2)].rearrange(
                            "b c n -> (b c) n")).then_inc(ld_p[slot], 16)
                elif pair.live():
                    slot = pair.off % 2
                    sp.wait_ge(y_done, pair.done(1, 1))
                    sp.dma_start(out[bass.ds(pair.g * BODY + 2 * pair.off, 2)].rearrange("b c n -> (b c) n"),
                                 y_out[:, slot, :]).then_inc(st_y[slot], 16)

            for k in range(3):
                load(At(0, BODY, k, NB))
            for n, w_ap, raw, s_ap, col in ((0, gate_w, gate_raw, gate_s, gs_col), (1, up_w, up_raw, up_s, us_col)):
                sp.dma_start(raw[:, 0:FT, :], w_ap[0:FT * P].rearrange("(k p) n -> p k n", p=P)).then_inc(ld_f, 16)
                sp.dma_start(tail_raw[n * TAIL:(n + 1) * TAIL, :], w_ap[FT * P:INTER]).then_inc(ld_f, 16)
                sp.dma_start(col[:, 0:FT], s_ap[0:FT * P].rearrange("(k p) -> p k", p=P),
                             allow_slow_non_contiguous=True).then_inc(ld_f, 16)
                sp.dma_start(ts_col[n * TAIL:(n + 1) * TAIL, :],
                             s_ap[FT * P:INTER].rearrange("(p a) -> p a", a=1)).then_inc(ld_f, 16)
            sp.dma_start(down_raw[:], down_w.rearrange("(k p) i -> p k i", p=P)).then_inc(ld_f, 16)
            sp.dma_start(ds_col[:], down_s.rearrange("(k p) -> p k", p=P),
                         allow_slow_non_contiguous=True).then_inc(ld_f, 16)
            for n in range(2):
                sp.dma_start(bout_col[n * D:(n + 1) * D, :], bout.rearrange("(p a) -> p a", a=1)).then_inc(ld_f, 16)
            walk(sp, step, LAST_FULL - 1)
            for slot in range(2):
                sp.wait_ge(st_y[slot], NPAIR // 2 * 16)

        N_SETUP = 4 + len(TILES) + 2 * (FT + 1)

        @block.tensor
        def _(pe):
            mm = nc.tensor.matmul
            n = 0

            def setup_bank():
                return ring[n % 2]

            def setup_free():
                if n >= 2:
                    pe.wait_ge(setup_ev, n - 1)

            pe.wait_ge(ld_w, 6 * 16)
            pe.wait_ge(const_done, 1)
            for h in range(H):
                last = mm(setup_bank()[:, h * D:(h + 1) * D], wk2[:, h].rearrange("d a c -> d (a c)"), wq_sb[:, h, :],
                          start=True, stop=True)
            last.then_inc(setup_mm, 1)
            n = 1
            for h in range(H):
                last = nc.tensor.transpose(setup_bank()[0:D, h * D:(h + 1) * D], wout_sb[:, h * D:(h + 1) * D],
                                           ident[0:D, 0:D])
            last.then_inc(setup_mm, 1)
            n = 2
            pe.wait_ge(setup_ev, 2)
            for h in range(H):
                last = mm(setup_bank()[:, h * D:(h + 1) * D], wv2[:, h].rearrange("d a c -> d (a c)"),
                          woutT[:, h * D:(h + 1) * D], start=True, stop=True)
            last.then_inc(setup_mm, 1)
            n = 3
            pe.wait_ge(tail_scaled, 2)
            for name in TILES:
                setup_free()
                src = tail_raw[:] if name == "t" else {"g": gate_raw, "u": up_raw}[name[0]][:, int(name[1]), :]
                for k in range(2):
                    last = nc.tensor.transpose(setup_bank()[:, k * P:(k + 1) * P], src[:, k * P:(k + 1) * P], ident[:])
                last.then_inc(setup_mm, 1)
                n += 1
            for k in range(FT + 1):
                setup_free()
                m = P if k < FT else TAIL
                for j in range(2):
                    last = nc.tensor.transpose(setup_bank()[0:m, j * P:(j + 1) * P], down_raw[:, j, k * P:k * P + m],
                                               ident[:])
                last.then_inc(setup_mm, 1)
                n += 1
            pe.wait_ge(setup_ev, n)
            pe.wait_ge(half_done, 2)

            def scores(e, u):
                slot, hg, jt = e.off % 4, u // 2, u % 2
                if u == 0:
                    pe.wait_ge(xlo_done, e.done(1, 1))
                    pe.wait_ge(mrow_done, e.done(1, 1))
                    pe.wait_ge(km_done, e.done(1, 1))
                wait(pe, exp_done, e.done(4, u - 1))
                for i in range(HG):
                    h = hg * HG + i
                    dst = s_bank[u % 2][:].rearrange("p b n -> p (b n)")[:, i * N:(i + 1) * N]
                    mm(dst, k_hl[:, slot, h, jt * P:(jt + 1) * P], x_hi[:, slot, :], start=True, stop=False)
                    last = mm(dst, k_hm[0:D + H, slot, h, jt * P:(jt + 1) * P], x_lom[0:D + H, slot, :],
                              start=False, stop=True)
                last.then_inc(s_mm, 1)

            def maxima(g, t, e, k):
                slot, it, hp = e.off % 4, k // 4, k % 4
                if k == 0:
                    pe.wait_ge(xhi_done, e.done(1, 1))
                if k in (0, 2):
                    pe.wait_ge(klo_done, e.done(4, k + 2))
                bank_free(pe, g, t, "mx", k)
                mm(bank(t, "mx", k)[:], x_hi[0:D, slot, it * P:(it + 1) * P],
                   k_hl[0:D, slot, 2 * hp:2 * hp + 2, :].rearrange("p h n -> p (h n)"),
                   start=True, stop=True).then_inc(mx_mm, 1)

            def attend(g, t, e, k):
                slot, hg, it = e.off % 4, k // 2, k % 2
                if it == 0:
                    pe.wait_ge(phi_done, e.done(4, 2 * hg + 2))
                    pe.wait_ge(plo_done, e.done(4, 2 * hg + 2))
                if k == 0:
                    pe.wait_ge(glo_done, e.done(2, 2))
                bank_free(pe, g, t, "av", k)
                for i in range(HG):
                    dst = bank(t, "av", k)[:, i * GW:(i + 1) * GW]
                    for jt in range(IT):
                        ph = p_hi[:, 2 * hg + jt, i, it * P:(it + 1) * P]
                        pl = p_lo[:, 2 * hg + jt, i, it * P:(it + 1) * P]
                        gh = g_hi[:, slot, jt, hg * HG + i, :]
                        gl = g_lo[:, slot, jt, hg * HG + i, :]
                        mm(dst, ph, gh, start=jt == 0, stop=False)
                        mm(dst[:, 0:D], ph, gl, start=False, stop=False)
                        last = mm(dst, pl, gh, start=False, stop=jt == IT - 1)
                last.then_inc(av_mm, 1)

            def keys(g, t, e, k):
                slot = e.off % 2
                if k == 0:
                    pe.wait_ge(chi_done, e.done(1, 1))
                    pe.wait_ge(clo_done, e.done(1, 1))
                bank_free(pe, g, t, "k", k)
                for j in range(2):
                    dst, w = bank(t, "k", k)[:, j * N:(j + 1) * N], a_w[:, (2 * k + j) * P:(2 * k + j + 1) * P]
                    mm(dst, w, c_hi[:, slot, :], start=True, stop=False)
                    last = mm(dst, w, c_lo[:, slot, :], start=False, stop=True)
                last.then_inc(k_mm, 1)

            def values(g, t, e, jt):
                slot = e.off % 2
                bank_free(pe, g, t, "g", jt)
                dst = bank(t, "g", jt)[:]
                mm(dst, c_hi[:, slot, jt * P:(jt + 1) * P], b_w[:], start=True, stop=False)
                mm(dst, c_lo[:, slot, jt * P:(jt + 1) * P], b_w[:], start=False, stop=True).then_inc(g_mm, 1)

            def max_rows(g, t, e):
                pe.wait_ge(mx_done, e.done(8, 8))
                bank_free(pe, g, t, "mt", 0)
                for it in range(IT):
                    last = nc.tensor.transpose(bank(t, "mt", 0)[0:H, it * P:(it + 1) * P], nmax[:, e.off % 2, it, :],
                                               ident[:])
                last.then_inc(mt_mm, 1)

            def y_rows(g, t, pr):
                pe.wait_ge(ad3_done, pr.done(2, 2))
                bank_free(pe, g, t, "yt", 0)
                for it in range(IT):
                    last = nc.tensor.transpose(bank(t, "yt", 0)[:, it * P:(it + 1) * P],
                                               yT[:, pr.off % 2, it].rearrange("p b c -> p (b c)"), ident[:])
                last.then_inc(yt_mm, 1)

            def xn2_cols(g, t, pr):
                pe.wait_ge(xn2_done, pr.done(1, 1))
                bank_free(pe, g, t, "xt", 0)
                for k in range(2):
                    last = nc.tensor.transpose(bank(t, "xt", 0)[:, k * P:(k + 1) * P], xn2[:, k * P:(k + 1) * P], ident[:])
                last.then_inc(xt_mm, 1)

            def gate_up(g, t, pr, r):
                if r == 0:
                    pe.wait_ge(xtlo_done, pr.done(1, 1))
                bank_free(pe, g, t, "r", r)
                for i, name in enumerate(ROUNDS[r]):
                    w, dst = TILES.index(name), bank(t, "r", r)[:, i * P:(i + 1) * P]
                    passes = [(a, b, k) for k in range(2) for a, b in ((gu_hi, xt_hi), (gu_lo, xt_hi), (gu_hi, xt_lo))]
                    for j, (a, b, k) in enumerate(passes):
                        last = mm(dst, a[:, k, w, :], b[:, k, :], start=j == 0, stop=j == len(passes) - 1)
                last.then_inc(r_mm, 1)

            def down(g, t, pr):
                pe.wait_ge(hhi_done, pr.done(3, 3))
                pe.wait_ge(hlo_done, pr.done(3, 3))
                bank_free(pe, g, t, "d", 0)
                passes = [(a, b, k) for k in range(FT + 1) for a, b in ((h_hi, dn_hi), (h_lo, dn_hi), (h_hi, dn_lo))]
                for j, (a, b, k) in enumerate(passes):
                    m = P if k < FT else TAIL
                    last = mm(bank(t, "d", 0)[:, 0:N], a[0:m, k, :], b[0:m, k, :], start=j == 0, stop=j == len(passes) - 1)
                last.then_inc(d_mm, 1)

            def step(g, t):
                e3 = stages(g, t)[3]
                for q, quarter in enumerate(uses(g, t)):
                    if e3.live():
                        scores(e3, q)
                    for kind, e, k in quarter:
                        if not e.live():
                            continue
                        if kind == "mx":
                            maxima(g, t, e, k)
                        elif kind == "av":
                            attend(g, t, e, k)
                        elif kind == "k":
                            keys(g, t, e, k)
                        elif kind == "g":
                            values(g, t, e, k)
                        elif kind == "mt":
                            max_rows(g, t, e)
                        elif kind == "yt":
                            y_rows(g, t, e)
                        elif kind == "xt":
                            xn2_cols(g, t, e)
                        elif kind == "r":
                            gate_up(g, t, e, k)
                        else:
                            down(g, t, e)

            walk(pe, step)

        @block.scalar
        def _(act):
            copy = lambda o, i: nc.scalar.activation(o, i, ACT.Copy)

            def exps(e, u):
                act.wait_ge(s_mm, e.done(4, u + 1))
                wait(act, plo_done, e.done(4, u - 1))
                nc.scalar.activation(p_f[:, u % 2].rearrange("p h n -> p (h n)"),
                                     s_bank[u % 2][:].rearrange("p b n -> p (b n)"), ACT.Exp).then_inc(exp_done, 1)

            def p_round(e, u):
                if not e.live():
                    return
                act.wait_ge(exp_done, e.done(4, u + 1))
                wait(act, av_mm, e.back(1).done(4, 2 * (u // 2) + 2))
                copy(p_hi[:, u].rearrange("p h n -> p (h n)"),
                     p_f[:, u % 2].rearrange("p h n -> p (h n)")).then_inc(phi_done, 1)

            def k_round(g, t, e, k):
                slot = e.off % 4
                act.wait_ge(k_mm, e.done(2, k + 1))
                wait(act, s_mm, e.back(4).done(4, 4))
                for odd in range(2):
                    src = bank(t, "k", k)[odd * D:(odd + 1) * D, :].rearrange("p (j n) -> p j n", j=2)
                    copy(k_hl[0:D, slot, 4 * k + odd:4 * k + 4:2, :], src).then_inc(khi_done, 1)

            def g_round(g, t, e, jt):
                slot = e.off % 4
                act.wait_ge(g_mm, e.done(2, jt + 1))
                wait(act, av_mm, e.back(4).done(4, 4))
                copy(g_hi[:, slot, jt, :, 0:D], bank(t, "g", jt)[:].rearrange("p (h d) -> p h d", h=H)).then_inc(ghi_done, 1)

            def max_row_copy(t, e):
                act.wait_ge(mt_mm, e.done(1, 1))
                wait(act, s_mm, e.back(4).done(4, 4))
                copy(x_lom[D:D + H, e.off % 4, :], bank(t, "mt", 0)[0:H, 0:N]).then_inc(mrow_done, 1)

            def c_round(e):
                act.wait_ge(ld_c[e.off % 4], e.landed(4, 32))
                wait(act, g_mm, e.back(2).done(2, 2))
                copy(c_hi[:, e.off % 2, :], c_in[:, e.off % 4, :]).then_inc(chi_done, 1)

            def x_round(e):
                act.wait_ge(xn_done, e.done(1, 1))
                wait(act, s_mm, e.back(4).done(4, 4))
                copy(x_hi[:, e.off % 4, :], xn[:, e.off % 2, :]).then_inc(xhi_done, 1)

            def xt_round(t, pr):
                act.wait_ge(xt_mm, pr.done(1, 1))
                wait(act, r_mm, pr.back(1).done(3, 3))
                copy(xt_hi[:].rearrange("p k n -> p (k n)"), bank(t, "xt", 0)[:, 0:N]).then_inc(xthi_done, 1)

            def tanh(t, pr, r):
                act.wait_ge(r_mm, pr.done(3, r + 1))
                wait(act, tg_done, pr.done(3, r - 1))
                nc.scalar.activation(th[:, r % 2].rearrange("p k n -> p (k n)"), bank(t, "r", r)[:, 0:2 * P], ACT.Tanh,
                                     scale=0.5 / SC).then_inc(th_done, 1)

            def h_round(pr, r):
                act.wait_ge(h_done, pr.done(3, r + 1))
                wait(act, d_mm, pr.back(1).done(1, 1))
                if r < 2:
                    copy(h_hi[:, 2 * r:2 * r + 2, :], h_f[:, r % 2]).then_inc(hhi_done, 1)
                else:
                    copy(h_hi[:, 4, :], h_f[:, 0, 0, :])
                    copy(h_hi[0:TAIL, 5, :], h_f[0:TAIL, 0, 1, :]).then_inc(hhi_done, 1)

            def step(g, t):
                e0, e1, e2, e3, e4, pr = stages(g, t)
                even, ffn = t % 2 == 0, pr.live()
                for q in range(4):
                    if e3.live():
                        exps(e3, q)
                    if q == 0:
                        p_round(e4, 3)
                        if e1.live():
                            x_round(e1)
                            k_round(g, t, e1, 0)
                        if ffn and not even:
                            h_round(pr, 0)
                            tanh(t, pr, 1)
                    elif q == 1:
                        if e3.live():
                            p_round(e3, 0)
                        if e1.live():
                            k_round(g, t, e1, 1)
                        if ffn and not even:
                            h_round(pr, 1)
                            tanh(t, pr, 2)
                    elif q == 2:
                        if e3.live():
                            p_round(e3, 1)
                        if e1.live():
                            g_round(g, t, e1, 0)
                        if ffn and not even:
                            h_round(pr, 2)
                        if ffn and even:
                            xt_round(t, pr)
                    else:
                        if e3.live():
                            p_round(e3, 2)
                        if e1.live():
                            g_round(g, t, e1, 1)
                        if e2.live():
                            max_row_copy(t, e2)
                        if e0.live():
                            c_round(e0)
                        if ffn and even:
                            tanh(t, pr, 0)

            walk(act, step)

        @block.vector
        def _(dve):
            V = nc.vector
            dve.wait_ge(ld_f, 12 * 16)
            for col in (gs_col[:, 0:FT], us_col[:, 0:FT], ts_col[:], ds_col[:]):
                last = V.tensor_scalar(col, col, SC, None, ALU.mult)
            last.then_inc(tail_scaled, 1)
            dve.wait_ge(tail_scaled, 1)
            for k in range(FT):
                V.tensor_scalar(gate_raw[:, k, :], gate_raw[:, k, :], gs_col[:, k:k + 1], None, ALU.mult)
                V.tensor_scalar(up_raw[:, k, :], up_raw[:, k, :], us_col[:, k:k + 1], None, ALU.mult)
            V.tensor_scalar(tail_raw[:], tail_raw[:], ts_col[:], None, ALU.mult)
            for k in range(2):
                last = V.tensor_scalar(down_raw[:, k, :], down_raw[:, k, :], ds_col[:, k:k + 1], None, ALU.mult)
            last.then_inc(tail_scaled, 1)

            n = 0

            def stacked(dst):
                dve.wait_ge(setup_mm, n + 1)
                V.tensor_copy(dst[:], ring[n % 2][:]).then_inc(weights_ready, 1)
                dve.wait_ge(weights_ready, 1 + n // 2)
                V.tensor_tensor(dst[D:P, :], ring[n % 2][D:P, :], dst[D:P, :], ALU.subtract).then_inc(setup_ev, 1)

            stacked(a_w)
            n = 1
            dve.wait_ge(setup_mm, 2)
            V.tensor_copy(woutT[:], ring[1][0:D, :]).then_inc(setup_ev, 1)
            n = 2
            stacked(b_w)
            n = 3
            halves = 2
            for i in range(len(TILES) + FT + 1):
                dve.wait_ge(setup_mm, n + 1)
                if i < len(TILES):
                    m, hi, lo = P, gu_hi[:, :, i, :], gu_lo[:, :, i, :]
                else:
                    k = i - len(TILES)
                    m = P if k < FT else TAIL
                    hi, lo = dn_hi[0:m, k, :].rearrange("p (a n) -> p a n", a=2), dn_lo[0:m, k, :].rearrange(
                        "p (a n) -> p a n", a=2)
                src = ring[n % 2][0:m, 0:N].rearrange("p (a n) -> p a n", a=2)
                V.tensor_copy(hi, src).then_inc(weights_ready, 1)
                halves += 1
                dve.wait_ge(weights_ready, halves)
                V.tensor_tensor(lo, src, hi, ALU.subtract).then_inc(setup_ev, 1)
                n += 1

            def max_reduce(t, e, k):
                it, hp = k // 4, k % 4
                dve.wait_ge(mx_mm, e.done(8, k + 1))
                if k == 0:
                    wait(dve, mt_mm, e.back(2).done(1, 1))
                V.tensor_reduce(nmax[:, e.off % 2, it, 2 * hp:2 * hp + 2],
                                bank(t, "mx", k)[:].rearrange("p (h n) -> p h n", h=2), AX_X, ALU.max,
                                negate=True).then_inc(mx_done, 1)

            def row_sums(t, e, k):
                dve.wait_ge(av_mm, e.done(4, k + 1))
                o = bank(t, "av", k)[:, 0:HG * GW].rearrange("p (h d) -> p h d", h=HG)
                V.reciprocal(rsum[:, k], o[:, :, D:GW]).then_inc(rs_done, 1)

            def normalise(t, e, k):
                hg, it = k // 2, k % 2
                o = bank(t, "av", k)[:, 0:HG * GW].rearrange("p (h d) -> p h d", h=HG)
                dve.wait_ge(rs_done, e.done(4, k + 1))
                if k == 0:
                    wait(dve, ad1_done, e.back(2).done(1, 1))
                V.tensor_tensor(heads[:, e.off % 2, hg * HG:(hg + 1) * HG, it, :], o[:, :, 0:D],
                                rsum[:, k].to_broadcast([P, HG, D]), ALU.mult).then_inc(av_done, 1)

            def k_rest(t, e, k):
                slot = e.off % 4
                for odd in range(2):
                    dve.wait_ge(khi_done, e.done(4, 2 * k + odd + 1))
                    src = bank(t, "k", k)[odd * D:(odd + 1) * D, :].rearrange("p (j n) -> p j n", j=2)
                    hs = slice(4 * k + odd, 4 * k + 4, 2)
                    V.tensor_tensor(k_hl[D:P, slot, hs, :], src, k_hl[0:D, slot, hs, :],
                                    ALU.subtract).then_inc(klo_done, 1)

            def k_copy(e):
                slot = e.off % 4
                dve.wait_ge(khi_done, e.done(4, 4))
                V.tensor_copy(k_hm[0:D, slot].rearrange("p h n -> p (h n)"),
                              k_hl[0:D, slot].rearrange("p h n -> p (h n)")).then_inc(km_done, 1)

            def g_rest(t, e, jt):
                slot = e.off % 4
                dve.wait_ge(ghi_done, e.done(2, jt + 1))
                V.tensor_tensor(g_lo[:, slot, jt, :, :], bank(t, "g", jt)[:].rearrange("p (h d) -> p h d", h=H),
                                g_hi[:, slot, jt, :, 0:D], ALU.subtract).then_inc(glo_done, 1)

            def ln_stats(e):
                dve.wait_ge(ld_x[e.off % 4], e.landed(4, 32))
                V.bn_stats(stats[:, e.off % 2, :], x_in[:, e.off % 4, :]).then_inc(st_done, 1)

            def ln_mean(e):
                V.bn_aggr(mv[:, e.off % 2, :], stats[:, e.off % 2, :]).then_inc(ag_done, 1)

            def ln_eps(e):
                dve.wait_ge(ag_done, e.done(1, 1))
                V.tensor_scalar(var[:, e.off % 2, :], mv[:, e.off % 2, 1:2], EPS, None, ALU.add).then_inc(va_done, 1)

            def ln_apply(e):
                dve.wait_ge(rstd_done, e.done(1, 1))
                wait(dve, xlo_done, e.back(2).done(1, 1))
                wait(dve, xhi_done, e.back(2).done(1, 1))
                V.tensor_scalar(xn[:, e.off % 2, :], x_in[:, e.off % 4, :], mv[:, e.off % 2, 0:1], rstd[:, e.off % 2, :],
                                ALU.subtract, ALU.mult).then_inc(xn_done, 1)

            def residual(t, pr):
                slot = pr.off % 2
                dve.wait_ge(yt_mm, pr.done(1, 1))
                dve.wait_ge(ld_p[slot], pr.landed(2, 16))
                V.scalar_tensor_tensor(out=x2[:, slot, :], in0=bank(t, "yt", 0)[:, 0:N], scalar=bout_col[:],
                                       in1=x_pair[:, slot, :], op0=ALU.add, op1=ALU.add).then_inc(x2_done, 1)

            def ln2(pr, part):
                slot = pr.off % 2
                if part == 0:
                    dve.wait_ge(x2_done, pr.done(1, 1))
                    V.bn_stats(stats2[:], x2[:, slot, :]).then_inc(st2_done, 1)
                elif part == 1:
                    V.bn_aggr(mv2[:], stats2[:]).then_inc(ag2_done, 1)
                elif part == 2:
                    dve.wait_ge(ag2_done, pr.done(1, 1))
                    V.tensor_scalar(var2[:], mv2[:, 1:2], EPS, None, ALU.add).then_inc(va2_done, 1)
                else:
                    dve.wait_ge(rstd2_done, pr.done(1, 1))
                    V.tensor_scalar(xn2[:], x2[:, slot, :], mv2[:, 0:1], rstd2[:], ALU.subtract,
                                    ALU.mult).then_inc(xn2_done, 1)

            def xt_rest(t, pr):
                dve.wait_ge(xthi_done, pr.done(1, 1))
                V.tensor_tensor(xt_lo[:].rearrange("p k n -> p (k n)"), bank(t, "xt", 0)[:, 0:N],
                                xt_hi[:].rearrange("p k n -> p (k n)"), ALU.subtract).then_inc(xtlo_done, 1)

            def silu_gate(t, pr, r):
                dve.wait_ge(th_done, pr.done(3, r + 1))
                flat = lambda v: v[:, r % 2].rearrange("p k n -> p (k n)")
                V.scalar_tensor_tensor(out=flat(tg), in0=flat(th), scalar=1.0, in1=bank(t, "r", r)[:, 0:2 * P],
                                       op0=ALU.add, op1=ALU.mult).then_inc(tg_done, 1)

            def times_up(t, pr, r):
                b, k = bank(t, "r", r), 0.5 / (SC * SC)
                dve.wait_ge(tg_done, pr.done(3, r + 1))
                if r == 0:
                    pre = pr.back(1).done(3, 3)
                else:
                    pre = pr.done(3, r - 1)
                wait(dve, hhi_done, pre)
                wait(dve, hlo_done, pre)
                if r < 2:
                    V.scalar_tensor_tensor(out=h_f[:, r % 2].rearrange("p k n -> p (k n)"),
                                           in0=tg[:, r % 2].rearrange("p k n -> p (k n)"), scalar=k,
                                           in1=b[:, 2 * P:4 * P], op0=ALU.mult, op1=ALU.mult).then_inc(h_done, 1)
                else:
                    V.scalar_tensor_tensor(out=h_f[:, 0, 0, :], in0=tg[:, 0, 0, :], scalar=k, in1=b[:, 2 * P:3 * P],
                                           op0=ALU.mult, op1=ALU.mult)
                    V.scalar_tensor_tensor(out=h_f[0:TAIL, 0, 1, :], in0=tg[0:TAIL, 0, 1, :], scalar=k,
                                           in1=b[TAIL:P, P:2 * P], op0=ALU.mult, op1=ALU.mult).then_inc(h_done, 1)

            def finish(t, pr):
                slot = pr.off % 2
                dve.wait_ge(d_mm, pr.done(1, 1))
                wait(dve, st_y[slot], pr.back(2).landed(2, 16))
                V.scalar_tensor_tensor(out=y_out[:, slot, :], in0=bank(t, "d", 0)[:, 0:N], scalar=1.0 / SC,
                                       in1=x2[:, slot, :], op0=ALU.mult, op1=ALU.add).then_inc(y_done, 1)

            def step(g, t):
                e0, e1, e2, e3, e4, pr = stages(g, t)
                even, ffn = t % 2 == 0, pr.live()
                if e2.live():
                    max_reduce(t, e2, 0)
                    max_reduce(t, e2, 1)
                if e4.live():
                    row_sums(t, e4, 1)
                if e1.live():
                    ln_apply(e1)
                if e2.live():
                    max_reduce(t, e2, 2)
                if e4.live():
                    normalise(t, e4, 1)
                if ffn and even:
                    residual(t, pr)
                if ffn and not even:
                    silu_gate(t, pr, 1)
                if e1.live():
                    k_rest(t, e1, 0)
                if ffn and even:
                    ln2(pr, 0)
                if ffn and not even:
                    times_up(t, pr, 1)
                if ffn and even:
                    dve.wait_ge(st2_done, pr.done(1, 1))
                if e2.live():
                    max_reduce(t, e2, 3)
                if ffn and even:
                    ln2(pr, 1)
                if e2.live():
                    max_reduce(t, e2, 4)
                if ffn and even:
                    ln2(pr, 2)
                if e4.live():
                    row_sums(t, e4, 2)
                if e2.live():
                    max_reduce(t, e2, 5)
                if e4.live():
                    normalise(t, e4, 2)
                if ffn and not even:
                    silu_gate(t, pr, 2)
                if e1.live():
                    k_rest(t, e1, 1)
                if ffn and not even:
                    times_up(t, pr, 2)
                if ffn and even:
                    ln2(pr, 3)
                if e2.live():
                    max_reduce(t, e2, 6)
                if e4.live():
                    row_sums(t, e4, 3)
                if e2.live():
                    max_reduce(t, e2, 7)
                if e4.live():
                    normalise(t, e4, 3)
                if e0.live():
                    ln_stats(e0)
                if e1.live():
                    k_copy(e1)
                    g_rest(t, e1, 0)
                if ffn and even:
                    xt_rest(t, pr)
                if e0.live():
                    dve.wait_ge(st_done, e0.done(1, 1))
                if e3.live():
                    row_sums(t, e3, 0)
                if e0.live():
                    ln_mean(e0)
                if e1.live():
                    g_rest(t, e1, 1)
                if e3.live():
                    normalise(t, e3, 0)
                if e0.live():
                    ln_eps(e0)
                if ffn and even:
                    silu_gate(t, pr, 0)
                    times_up(t, pr, 0)
                if ffn and not even:
                    finish(t, pr)

            walk(dve, step)

        @block.gpsimd
        def _(pool):
            G = nc.gpsimd
            G.memset(ident[:], 0.0).then_inc(memset_done, 1)
            pool.wait_ge(memset_done, 1)
            G.affine_select(out=ident[:], in_=ident[:], compare_op=ALU.not_equal, fill=1.0, base=0,
                            pattern=[[-1, P]], channel_multiplier=1).then_inc(const_done, 1)
            pool.wait_ge(const_done, 1)
            G.memset(k_hm[D:D + H].rearrange("p s h n -> p (s h n)").bitcast(F32), 0.0).then_inc(memset_done, 1)
            pool.wait_ge(memset_done, 2)
            for slot in range(4):
                v = k_hm[D:D + H, slot]
                last = G.affine_select(out=v, in_=v, compare_op=ALU.not_equal, fill=1.0, base=0,
                                       pattern=[[-1, H], [0, N]], channel_multiplier=1)
            last.then_inc(half_done, 1)
            pool.wait_ge(half_done, 1)
            G.memset(g_hi[:, :, :, :, D:GW], 1.0)
            G.memset(neg_half[:], -0.5).then_inc(half_done, 1)
            pool.wait_ge(half_done, 2)

            def p_rest(e, u):
                if not e.live():
                    return
                pool.wait_ge(phi_done, e.done(4, u + 1))
                flat = lambda v: v.rearrange("p h n -> p (h n)")
                G.tensor_tensor(flat(p_lo[:, u]), flat(p_f[:, u % 2]), flat(p_hi[:, u]),
                                ALU.subtract).then_inc(plo_done, 1)

            def head_sum(e, part):
                slot = e.off % 2
                if part == 0:
                    pool.wait_ge(av_done, e.done(4, 4))
                    G.tensor_tensor(half[:], heads[:, slot, 0:4], heads[:, slot, 4:8], ALU.add).then_inc(ad1_done, 1)
                elif part == 1:
                    pool.wait_ge(ad1_done, e.done(1, 1))
                    G.tensor_tensor(quar[:], half[:, 0:2], half[:, 2:4], ALU.add).then_inc(ad2_done, 1)
                else:
                    pool.wait_ge(ad2_done, e.done(1, 1))
                    wait(pool, yt_mm, At(e.g, 2, (e.off // 2) - 2, NPAIR).done(1, 1))
                    G.tensor_tensor(yT[:, e.off // 2 % 2, :, e.off % 2, :], quar[:, 0], quar[:, 1],
                                    ALU.add).then_inc(ad3_done, 1)

            def step(g, t):
                e0, e1, e2, e3, e4, pr = stages(g, t)
                even, ffn = t % 2 == 0, pr.live()
                p_rest(e4, 3)
                if e1.live():
                    pool.wait_ge(xhi_done, e1.done(1, 1))
                    G.tensor_tensor(x_lom[0:D, e1.off % 4, :], xn[0:D, e1.off % 2, :], x_hi[0:D, e1.off % 4, :],
                                    ALU.subtract).then_inc(xlo_done, 1)
                if ffn and not even:
                    h_rest(pr, 0)
                p_rest(e3, 0) if e3.live() else None
                if ffn and even:
                    pool.wait_ge(va2_done, pr.done(1, 1))
                    G.tensor_tensor(rstd2[:], var2[:], neg_half[:], ALU.pow).then_inc(rstd2_done, 1)
                if ffn and not even:
                    h_rest(pr, 1)
                if e3.live():
                    p_rest(e3, 1)
                if ffn and not even:
                    h_rest(pr, 2)
                if e4.live():
                    head_sum(e4, 0)
                    head_sum(e4, 1)
                    head_sum(e4, 2)
                if e3.live():
                    p_rest(e3, 2)
                if e0.live():
                    pool.wait_ge(chi_done, e0.done(1, 1))
                    G.tensor_tensor(c_lo[:, e0.off % 2, :], c_in[:, e0.off % 4, :], c_hi[:, e0.off % 2, :],
                                    ALU.subtract).then_inc(clo_done, 1)
                    pool.wait_ge(va_done, e0.done(1, 1))
                    G.tensor_tensor(rstd[:, e0.off % 2, :], var[:, e0.off % 2, :], neg_half[:],
                                    ALU.pow).then_inc(rstd_done, 1)

            def h_rest(pr, r):
                pool.wait_ge(hhi_done, pr.done(3, r + 1))
                if r < 2:
                    G.tensor_tensor(h_lo[:, 2 * r:2 * r + 2, :], h_f[:, r % 2], h_hi[:, 2 * r:2 * r + 2, :],
                                    ALU.subtract).then_inc(hlo_done, 1)
                else:
                    G.tensor_tensor(h_lo[:, 4, :], h_f[:, 0, 0, :], h_hi[:, 4, :], ALU.subtract)
                    G.tensor_tensor(h_lo[0:TAIL, 5, :], h_f[0:TAIL, 0, 1, :], h_hi[0:TAIL, 5, :],
                                    ALU.subtract).then_inc(hlo_done, 1)

            walk(pool, step)


_INS = ["x", "ctx_2048", "L0_xattn_Wq", "L0_xattn_Wkv", "L0_xattn_Wout", "L0_xattn_bout", "L0_ffn_gate_w",
        "L0_ffn_up_w", "L0_ffn_down_w", "L0_ffn_gate_s", "L0_ffn_up_s", "L0_ffn_down_s"]


def kernel(**inputs):
    import numpy as _np
    import concourse.bacc as _bacc
    from concourse import mybir as _mybir
    from concourse.bass_utils import run_bass_kernel_spmd as _run

    nc = _bacc.Bacc("TRN2", target_bir_lowering=False, num_devices=1)
    arrays, args = {}, []
    for name in _INS:
        a = _np.ascontiguousarray(inputs[name])
        arrays[f"in_{name}_dram"] = a
        args.append(nc.dram_tensor(f"in_{name}_dram", a.shape, _mybir.dt.from_np(a.dtype), kind="ExternalInput").ap())
    dt = _mybir.dt.from_np(_np.dtype("float32"))
    args.append(nc.dram_tensor("out_dram", inputs["x"].shape, dt, kind="ExternalOutput").ap())
    xattn_ffn(nc, *args)
    r = _run(nc, [arrays], core_ids=[0])
    return r.results[0]["out_dram"]
```

```python
from contextlib import ExitStack

import concourse.bass as bass
from concourse import mybir

ALU = mybir.AluOpType
ACT = mybir.ActivationFunctionType
F32 = mybir.dt.float32
F16 = mybir.dt.float16
AX_X = mybir.AxisListType.X

P = 128
EPS = 1e-5
SC = 16.0
BODY = 4


def orders(text):
    items = []
    for token in text.split():
        name, place = token.split("@")
        kind, _, what = name.partition(":")
        lag, _, bank = place.partition("/")
        part = what.rstrip("ab")
        items.append((kind, int(part or 0), what[len(part):], int(lag), int(bank or -1)))
    return items


PE_ORDER = orders("""
    k:0a@0/2 gu:0@3/3 mt:b@1/4 k:0b@0/0 mx:0a@0/1 k:1a@0/5 s:6a@1/6 s:7a@1/7 av:2b@2/2 k:1b@0/1 av:3b@2/4
    mx:1a@0/0 s:0b@1/6 s:1b@1/7 g:0a@0/5 gu:1@3/2 s:2b@1/6 s:3b@1/7 mx:2a@0/1 mx:3a@0/4 g:1a@0/3 g:0b@0/0
    mx:4a@0/2 s:4b@1/6 mx:0b@0/4 mx:5a@0/1 s:5b@1/7 mx:6a@0/5 s:6b@1/6 mx:7a@0/2 down@4/0 mt:a@0/5 g:1b@0/1
    mx:1b@0/2 s:7b@1/7 yt@2/5 s:0a@0/6 av:0a@1/3 av:1a@1/0 s:1a@0/7 mx:2b@0/1 s:2a@0/6 mx:3b@0/5 mx:4b@0/4
    av:2a@1/0 av:3a@1/3 av:0b@1/1 s:3a@0/7 s:4a@0/6 mx:5b@0/4 gu:2@3/5 xt@2/2 av:1b@1/0 mx:6b@0/1 s:5a@0/7
    mx:7b@0/4
""")
ACT_ORDER = orders("""
    h_hi:0@4 p_hi:2b@2 c_hi:a@0 p_hi:3b@2 exp:1a@1 c_hi:b@0 exp:2a@1 p_hi:0a@1 exp:3a@1 exp:4a@1 h_hi:1@4
    xt_hi@3 p_hi:1a@1 exp:5a@1 tanh:2@4 k_hi:0a@0 x_hi:a@0 max_row:b@1 k_hi:0b@0 k_hi:1a@0 exp:6a@1 exp:7a@1
    h_hi:2@4 k_hi:1b@0 exp:0b@1 exp:1b@1 tanh:0@3 g_hi:0a@0 tanh:1@3 x_hi:b@0 p_hi:0b@1 exp:2b@1 exp:3b@1
    g_hi:0b@0 exp:4b@1 p_hi:2a@1 g_hi:1a@0 p_hi:3a@1 exp:5b@1 exp:6b@1 max_row:a@0 g_hi:1b@0 p_hi:1b@1 exp:7b@1
    exp:0a@0
""")
DVE_ORDER = orders("""
    rsum:1b@3 max:6b@2 norm:1b@3 max:7b@2 stats:a@0 gate:2@5 xn:b@1 up:2@5 k_lo:0a@1 max:0a@1 k_lo:0b@1
    rsum:2b@3 k_lo:1a@1 norm:2b@3 rsum:3b@3 k_lo:1b@1 norm:3b@3 max:1a@1 stats:b@0 gate:0@4 gate:1@4 up:0@4
    up:1@4 max:3a@1 max:2a@1 g_lo:0a@1 max:4a@1 g_lo:0b@1 max:6a@1 max:7a@1 max:5a@1 k_copy:a@1 finish@5
    g_lo:1a@1 k_copy:b@1 g_lo:1b@1 mean:a@0 x2@3 max:0b@1 mean:b@0 rsum:0a@2 eps:a@0 rsum:1a@2 stats2@3
    norm:1a@2 mean2@3 norm:0a@2 eps2@3 max:2b@1 max:4b@1 max:3b@1 max:1b@1 eps:b@0 rsum:2a@2 rsum:3a@2 rsum:0b@2
    xn2@3 norm:2a@2 norm:0b@2 norm:3a@2 max:5b@1 xn:a@0 xt_lo@3
""")
POOL_ORDER = orders("""
    sum:2b@3 p_lo:2a@2 p_lo:3a@2 p_lo:1b@2 h_lo:0@4 c_lo:a@0 rstd2@3 p_lo:2b@2 rstd:a@0 rstd:b@0 c_lo:b@0
    p_lo:3b@2 p_lo:0a@1 sum:0a@2 p_lo:1a@1 h_lo:1@4 h_lo:2@4 sum:1a@2 x_lo:a@0 sum:0b@2 x_lo:b@0 sum:2a@2
    sum:1b@2 p_lo:0b@1
""")

class At:

    def __init__(self, g, per, off, total):
        self.g, self.per, self.off, self.total = g, per, off, total

    def live(self):
        return not isinstance(self.g, int) or 0 <= self.per * self.g + self.off < self.total

    def back(self, k):
        return At(self.g, self.per, self.off - k, self.total)

    def landed(self, slots, inc):
        if isinstance(self.g, int):
            return ((self.per * self.g + self.off) // slots + 1) * inc
        return self.g * (self.per // slots * inc) + (self.off // slots + 1) * inc


def wait(eng, sem, value):
    if not isinstance(value, int) or value > 0:
        eng.wait_ge(sem, value)


def xattn_ffn(nc, x, ctx_in, wq, wkv, wout, bout, gate_w, up_w, down_w, gate_s, up_s, down_s, out):
    NB, C, N = x.shape
    HID = wq.shape[0]
    D = 64
    H = HID // D
    INTER = gate_w.shape[0]
    NPAIR = NB // 2
    IT = N // P
    FT = INTER // P
    TAIL = INTER - FT * P
    assert C == D == 64 and N == 256 and H == 8 and FT == 5 and TAIL == 64
    HC = H * D
    GW = D + 1
    HG = H // 2
    ROUNDS = [["g0", "g1", "u0", "u1"], ["g2", "g3", "u2", "u3"], ["g4", "t", "u4"]]
    TILES = [name for r in ROUNDS for name in r]

    with ExitStack() as stack:
        def sb(name, shape, dt=F32):
            return stack.enter_context(nc.sbuf_tensor(name, shape, dt))

        def psum(name, shape):
            return stack.enter_context(nc.psum_tensor(name, shape, F32))

        def sem(name):
            return stack.enter_context(nc.semaphore(name))

        ident = sb("ident", [P, P])
        neg_half = sb("neg_half", [P, 1])
        wq_sb = sb("wq_sb", [D, H, D])
        wout_sb = sb("wout_sb", [D, HC])
        woutT = sb("woutT", [D, HC])
        tail_raw = sb("tail_raw", [P, N])
        gs_col = sb("gs_col", [P, FT + 1])
        us_col = sb("us_col", [P, FT + 1])
        ts_col = sb("ts_col", [P, 1])
        ds_col = sb("ds_col", [P, 2])
        bout_col = sb("bout_col", [P, 1])
        a_w = sb("a_w", [P, HC], F16)
        b_w = sb("b_w", [P, HC], F16)
        gu_hi = sb("gu_hi", [P, 2, len(TILES), P], F16)
        gu_lo = sb("gu_lo", [P, 2, len(TILES), P], F16)
        dn_hi = sb("dn_hi", [P, FT + 1, N], F16)
        dn_lo = sb("dn_lo", [P, FT + 1, N], F16)
        x_in = sb("x_in", [P, 4, N])
        c_in = sb("c_in", [P, 4, N])
        c_hi = sb("c_hi", [P, 2, N], F16)
        c_lo = sb("c_lo", [P, 2, N], F16)
        stats = sb("stats", [P, 2, 6])
        mv = sb("mv", [P, 2, 2])
        var = sb("var", [P, 2, 1])
        rstd = sb("rstd", [P, 2, 1])
        xn = sb("xn", [P, 2, N])
        x_hi = sb("x_hi", [P, 4, N], F16)
        x_lom = sb("x_lom", [P, 4, N], F16)
        k_hl = sb("k_hl", [P, 4, H, N], F16)
        k_hm = sb("k_hm", [P, 4, H, N], F16)
        g_hi = sb("g_hi", [P, 4, IT, H, GW], F16)
        g_lo = sb("g_lo", [P, 4, IT, H, D], F16)
        nmax = sb("nmax", [P, 2, IT, H])
        p_f = sb("p_f", [P, 2, 4, HG, N])
        p_hi = sb("p_hi", [P, 2, 4, HG, N], F16)
        p_lo = sb("p_lo", [P, 2, 4, HG, N], F16)
        raw = p_f[:].rearrange("p e u h n -> p (e u h n)")
        at = 0

        def raw_part(m, *shape):
            nonlocal at
            size = 1
            for n in shape:
                size *= n
            names = " ".join(f"d{i}" for i in range(len(shape)))
            view = raw[0:m, at:at + size].rearrange(f"p ({names}) -> p {names}",
                                                    **{f"d{i}": n for i, n in enumerate(shape)})
            at += size
            return view

        gate_raw, up_raw = raw_part(P, FT + 1, N), raw_part(P, FT + 1, N)
        down_raw = raw_part(P, 2, INTER)
        wk2, wv2 = raw_part(D, H, 2, D), raw_part(D, H, 2, D)
        rsum = sb("rsum", [P, 2, 4, HG, 1])
        heads = sb("heads", [P, 2, H, IT, D])
        half = sb("half", [P, 2, 4, IT, D])
        quar = sb("quar", [P, 2, 2, IT, D])
        yT = sb("yT", [P, 2, IT, 2, D])
        x_pair = sb("x_pair", [P, 2, N])
        x2 = sb("x2", [P, 2, N])
        stats2 = sb("stats2", [P, 6])
        mv2 = sb("mv2", [P, 2])
        var2 = sb("var2", [P, 1])
        rstd2 = sb("rstd2", [P, 1])
        xn2 = sb("xn2", [P, N])
        xt_hi = sb("xt_hi", [P, 2, P], F16)
        xt_lo = sb("xt_lo", [P, 2, P], F16)
        th = sb("th", [P, 3, 2, P])
        tg = sb("tg", [P, 3, 2, P])
        h_f = sb("h_f", [P, 3, 2, P])
        h_hi = sb("h_hi", [P, FT + 1, P], F16)
        h_lo = sb("h_lo", [P, FT + 1, P], F16)
        y_out = sb("y_out", [P, 2, N])

        bank = [psum(f"bank{i}", [P, 512]) for i in range(8)]


        ld_w, ld_f = sem("ld_w"), sem("ld_f")
        ld_x = [sem(f"ld_x{i}") for i in range(4)]
        ld_c = [sem(f"ld_c{i}") for i in range(4)]
        ld_p = [sem(f"ld_p{i}") for i in range(2)]
        st_y = [sem(f"st_y{i}") for i in range(2)]
        memset_done, const_done, half_done = sem("memset_done"), sem("const_done"), sem("half_done")
        setup_mm, setup_ev = sem("setup_mm"), sem("setup_ev")
        tail_scaled = sem("tail_scaled")
        weights_ready = sem("weights_ready")
        done = {kind: sem(f"{kind}_done") for order in (PE_ORDER, ACT_ORDER, DVE_ORDER, POOL_ORDER)
                for kind in sorted({item[0] for item in order})}

        PLACES = {}
        for order in (PE_ORDER, ACT_ORDER, DVE_ORDER, POOL_ORDER):
            for position, (kind, k, who, lag, _) in enumerate(order):
                PLACES.setdefault(kind, {})[k, who] = (lag, position)
        BANK = {(kind, k, who): number for kind, k, who, _, number in PE_ORDER}

        def whose(e):
            return "" if e.per == 2 else "ab"[e.off % 2]

        def period(e):
            return e.off if e.per == 2 else e.off // 2

        def count(kind, e, k=0):
            places = PLACES[kind]
            lag, position = places[k, whose(e)]
            ahead = [period(e) + lag - other - (after > position) + 1 for other, after in places.values()]

            def at(g):
                return sum(min(max(2 * g + n, 0), NPAIR) for n in ahead)

            if isinstance(e.g, int):
                return at(e.g) if 2 * e.g + period(e) >= 0 else 0
            steady = sum(ahead)
            for g in (FIRST_FULL, LAST_FULL - 1):
                assert 2 * g + period(e) >= 0 and at(g) == 2 * len(ahead) * g + steady, (kind, k)
            return e.g * (2 * len(ahead)) + steady

        def final(kind, e, parts):
            return max(parts, key=lambda k: PLACES[kind][k, whose(e)])

        def first(kind, e):
            return min((k for k, who in PLACES[kind] if who == whose(e)), key=lambda k: PLACES[kind][k, whose(e)])

        def in_bank(kind, e, k=0):
            return bank[BANK[kind, k, whose(e)]]

        def work(g, t, item):
            _, _, who, lag, _ = item
            if who:
                return At(g, 4, 2 * (t - lag) + "ab".index(who), NB)
            return At(g, 2, t - lag, NPAIR)

        READER = {"mx": "max", "av": "norm", "k": "k_lo", "g": "g_lo", "mt": "max_row", "yt": "x2", "xt": "xt_lo",
                  "gu": "up", "d": "finish", "s": "exp", "down": "finish"}

        def bank_free(pe, g, t, position):
            number, before = PE_ORDER[position][4], position
            while True:
                before -= 1
                if before < 0:
                    before += len(PE_ORDER)
                    t -= 1
                if isinstance(g, int) and 2 * g + t < 0:
                    return
                kind, k, _, _, other = PE_ORDER[before]
                e = work(g, t, PE_ORDER[before])
                if other == number and e.live():
                    wait(pe, done[READER[kind]], count(READER[kind], e, k))
                    return

        block = stack.enter_context(nc.Block())

        LAG_END = max(item[3] for order in (PE_ORDER, ACT_ORDER, DVE_ORDER, POOL_ORDER) for item in order)
        GROUPS = (NPAIR + LAG_END + 1) // 2
        FIRST_FULL = 5
        LAST_FULL = NPAIR // 2

        def walk(eng, step, last_full=LAST_FULL):
            for g in range(FIRST_FULL):
                for t in range(2):
                    step(g, t)
            with eng.Fori(FIRST_FULL, last_full) as g:
                for t in range(2):
                    step(g, t)
            for g in range(last_full, GROUPS):
                for t in range(2):
                    step(g, t)

        @block.sync
        def _(sp):
            kv = wkv.rearrange("(s h d) c -> s d h c", s=2, d=D)
            for c in range(2):
                sp.dma_start(wk2[:, :, c, :], kv[0]).then_inc(ld_w, 16)
                sp.dma_start(wv2[:, :, c, :], kv[1]).then_inc(ld_w, 16)
            sp.dma_start(wq_sb[:], wq.rearrange("(h d) c -> d h c", d=D)).then_inc(ld_w, 16)
            sp.dma_start(wout_sb[:], wout).then_inc(ld_w, 16)

            def load(e):
                if not e.live():
                    return
                slot = e.off % 4
                src_x, src_c = (v[bass.ds(e.g * BODY + e.off, 1)].rearrange("b c n -> (b c) n") for v in (x, ctx_in))
                wait(sp, done["xn"], count("xn", e.back(4)))
                for lo in (0, D):
                    sp.dma_start(x_in[lo:lo + D, slot, :], src_x).then_inc(ld_x[slot], 16)
                wait(sp, done["c_lo"], count("c_lo", e.back(4)))
                for lo in (0, D):
                    sp.dma_start(c_in[lo:lo + D, slot, :], src_c).then_inc(ld_c[slot], 16)

            STORE_LAG = PLACES["finish"][0, ""][0]

            def step(g, t):
                load(At(g, 4, 2 * t + 2, NB))
                load(At(g, 4, 2 * t + 3, NB))
                nxt = At(g, 2, t - 1, NPAIR)
                if nxt.live():
                    slot = nxt.off % 2
                    wait(sp, done["x2"], count("x2", nxt.back(2)))
                    sp.dma_start(x_pair[:, slot, :], x[bass.ds(nxt.g * BODY + 2 * nxt.off, 2)].rearrange(
                        "b c n -> (b c) n")).then_inc(ld_p[slot], 16)
                last = At(g, 2, t - STORE_LAG, NPAIR)
                if last.live():
                    slot = last.off % 2
                    sp.wait_ge(done["finish"], count("finish", last))
                    sp.dma_start(out[bass.ds(last.g * BODY + 2 * last.off, 2)].rearrange("b c n -> (b c) n"),
                                 y_out[:, slot, :]).then_inc(st_y[slot], 16)

            for k in range(2):
                load(At(0, BODY, k, NB))
            for n, w_ap, raw, s_ap, col in ((0, gate_w, gate_raw, gate_s, gs_col), (1, up_w, up_raw, up_s, us_col)):
                sp.dma_start(raw[:, 0:FT, :], w_ap[0:FT * P].rearrange("(k p) n -> p k n", p=P)).then_inc(ld_f, 16)
                sp.dma_start(tail_raw[n * TAIL:(n + 1) * TAIL, :], w_ap[FT * P:INTER]).then_inc(ld_f, 16)
                sp.dma_start(col[:, 0:FT], s_ap[0:FT * P].rearrange("(k p) -> p k", p=P),
                             allow_slow_non_contiguous=True).then_inc(ld_f, 16)
                sp.dma_start(ts_col[n * TAIL:(n + 1) * TAIL, :],
                             s_ap[FT * P:INTER].rearrange("(p a) -> p a", a=1)).then_inc(ld_f, 16)
            sp.dma_start(down_raw[:], down_w.rearrange("(k p) i -> p k i", p=P)).then_inc(ld_f, 16)
            sp.dma_start(ds_col[:], down_s.rearrange("(k p) -> p k", p=P),
                         allow_slow_non_contiguous=True).then_inc(ld_f, 16)
            for n in range(2):
                sp.dma_start(bout_col[n * D:(n + 1) * D, :], bout.rearrange("(p a) -> p a", a=1)).then_inc(ld_f, 16)
            walk(sp, step, LAST_FULL - 1)
            for slot in range(2):
                sp.wait_ge(st_y[slot], NPAIR // 2 * 16)

        N_SETUP = 4 + len(TILES) + 2 * (FT + 1)

        @block.tensor
        def _(pe):
            mm = nc.tensor.matmul
            n = 0

            def setup_bank():
                return bank[n % 2]

            def setup_free():
                if n >= 2:
                    pe.wait_ge(setup_ev, n - 1)

            pe.wait_ge(ld_w, 6 * 16)
            pe.wait_ge(const_done, 1)
            for h in range(H):
                last = mm(setup_bank()[:, h * D:(h + 1) * D], wk2[:, h].rearrange("d a c -> d (a c)"), wq_sb[:, h, :],
                          start=True, stop=True)
            last.then_inc(setup_mm, 1)
            n = 1
            for h in range(H):
                last = nc.tensor.transpose(setup_bank()[0:D, h * D:(h + 1) * D], wout_sb[:, h * D:(h + 1) * D],
                                           ident[0:D, 0:D])
            last.then_inc(setup_mm, 1)
            n = 2
            pe.wait_ge(setup_ev, 2)
            for h in range(H):
                last = mm(setup_bank()[:, h * D:(h + 1) * D], wv2[:, h].rearrange("d a c -> d (a c)"),
                          woutT[:, h * D:(h + 1) * D], start=True, stop=True)
            last.then_inc(setup_mm, 1)
            n = 3
            pe.wait_ge(tail_scaled, 2)
            for name in TILES:
                setup_free()
                src = tail_raw[:] if name == "t" else {"g": gate_raw, "u": up_raw}[name[0]][:, int(name[1]), :]
                for k in range(2):
                    last = nc.tensor.transpose(setup_bank()[:, k * P:(k + 1) * P], src[:, k * P:(k + 1) * P], ident[:])
                last.then_inc(setup_mm, 1)
                n += 1
            for k in range(FT + 1):
                setup_free()
                m = P if k < FT else TAIL
                for j in range(2):
                    last = nc.tensor.transpose(setup_bank()[0:m, j * P:(j + 1) * P], down_raw[:, j, k * P:k * P + m],
                                               ident[:])
                last.then_inc(setup_mm, 1)
                n += 1
            pe.wait_ge(setup_ev, n)
            pe.wait_ge(half_done, 2)

            def scores(e, k, dst):
                slot, hg, jt = e.off % 4, k // 4, k // 2 % 2
                if k == first("s", e):
                    pe.wait_ge(done["x_lo"], count("x_lo", e))
                    pe.wait_ge(done["max_row"], count("max_row", e))
                    pe.wait_ge(done["k_copy"], count("k_copy", e))
                    pe.wait_ge(done["k_lo"], count("k_lo", e, final("k_lo", e, range(2))))
                for i in range(2):
                    h = hg * HG + k % 2 * 2 + i
                    col = slice(i * N, (i + 1) * N)
                    mm(dst[:, col], k_hl[:, slot, h, jt * P:(jt + 1) * P], x_hi[:, slot, :], start=True, stop=False)
                    last = mm(dst[:, col], k_hm[0:D + H, slot, h, jt * P:(jt + 1) * P], x_lom[0:D + H, slot, :],
                              start=False, stop=True)
                last.then_inc(done["s"], 1)

            def maxima(e, k, dst):
                slot, it, hp = e.off % 4, k // 4, k % 4
                pe.wait_ge(done["x_hi"], count("x_hi", e))
                pe.wait_ge(done["k_hi"], count("k_hi", e, hp // 2))
                mm(dst[:], x_hi[0:D, slot, it * P:(it + 1) * P],
                   k_hl[0:D, slot, 2 * hp:2 * hp + 2, :].rearrange("p h n -> p (h n)"),
                   start=True, stop=True).then_inc(done["mx"], 1)

            def attend(e, k, dst):
                slot, hg, it = e.off % 4, k // 2, k % 2
                pe.wait_ge(done["p_lo"], count("p_lo", e, final("p_lo", e, (2 * hg, 2 * hg + 1))))
                if k == first("av", e):
                    pe.wait_ge(done["g_lo"], count("g_lo", e, final("g_lo", e, range(2))))
                for i in range(HG):
                    o = dst[:, i * GW:(i + 1) * GW]
                    for jt in range(IT):
                        ph = p_hi[:, e.off % 2, 2 * hg + jt, i, it * P:(it + 1) * P]
                        pl = p_lo[:, e.off % 2, 2 * hg + jt, i, it * P:(it + 1) * P]
                        gh = g_hi[:, slot, jt, hg * HG + i, :]
                        gl = g_lo[:, slot, jt, hg * HG + i, :]
                        mm(o, ph, gh, start=jt == 0, stop=False)
                        mm(o[:, 0:D], ph, gl, start=False, stop=False)
                        last = mm(o, pl, gh, start=False, stop=jt == IT - 1)
                last.then_inc(done["av"], 1)

            def keys(e, k, dst):
                slot = e.off % 2
                pe.wait_ge(done["c_lo"], count("c_lo", e))
                for j in range(2):
                    o, w = dst[:, j * N:(j + 1) * N], a_w[:, (2 * k + j) * P:(2 * k + j + 1) * P]
                    mm(o, w, c_hi[:, slot, :], start=True, stop=False)
                    last = mm(o, w, c_lo[:, slot, :], start=False, stop=True)
                last.then_inc(done["k"], 1)

            def values(e, jt, dst):
                slot = e.off % 2
                pe.wait_ge(done["c_lo"], count("c_lo", e))
                mm(dst[:], c_hi[:, slot, jt * P:(jt + 1) * P], b_w[:], start=True, stop=False)
                mm(dst[:], c_lo[:, slot, jt * P:(jt + 1) * P], b_w[:], start=False, stop=True).then_inc(done["g"], 1)

            def max_rows(e, k, dst):
                pe.wait_ge(done["max"], count("max", e, final("max", e, range(8))))
                for it in range(IT):
                    last = nc.tensor.transpose(dst[0:H, it * P:(it + 1) * P], nmax[:, e.off % 2, it, :], ident[:])
                last.then_inc(done["mt"], 1)

            def y_rows(pr, k, dst):
                for odd in range(2):
                    pe.wait_ge(done["sum"], count("sum", At(pr.g, 4, 2 * pr.off + odd, NB), 2))
                for it in range(IT):
                    last = nc.tensor.transpose(dst[:, it * P:(it + 1) * P],
                                               yT[:, pr.off % 2, it].rearrange("p b c -> p (b c)"), ident[:])
                last.then_inc(done["yt"], 1)

            def xn2_cols(pr, k, dst):
                pe.wait_ge(done["xn2"], count("xn2", pr))
                for j in range(2):
                    last = nc.tensor.transpose(dst[:, j * P:(j + 1) * P], xn2[:, j * P:(j + 1) * P], ident[:])
                last.then_inc(done["xt"], 1)

            def gate_up(pr, r, dst):
                pe.wait_ge(done["xt_lo"], count("xt_lo", pr))
                for i, name in enumerate(ROUNDS[r]):
                    w, o = TILES.index(name), dst[:, i * P:(i + 1) * P]
                    passes = [(a, b, j) for j in range(2) for a, b in ((gu_hi, xt_hi), (gu_lo, xt_hi), (gu_hi, xt_lo))]
                    for n, (a, b, j) in enumerate(passes):
                        last = mm(o, a[:, j, w, :], b[:, j, :], start=n == 0, stop=n == len(passes) - 1)
                last.then_inc(done["gu"], 1)

            def down(pr, k, dst):
                pe.wait_ge(done["h_lo"], count("h_lo", pr, final("h_lo", pr, range(3))))
                passes = [(a, b, j) for j in range(FT + 1) for a, b in ((h_hi, dn_hi), (h_lo, dn_hi), (h_hi, dn_lo))]
                for n, (a, b, j) in enumerate(passes):
                    m = P if j < FT else TAIL
                    last = mm(dst[:, 0:N], a[0:m, j, :], b[0:m, j, :], start=n == 0, stop=n == len(passes) - 1)
                last.then_inc(done["down"], 1)

            does = {"s": scores, "mx": maxima, "av": attend, "k": keys, "g": values, "mt": max_rows, "yt": y_rows,
                    "xt": xn2_cols, "gu": gate_up, "down": down}

            def step(g, t):
                for position, item in enumerate(PE_ORDER):
                    e = work(g, t, item)
                    if e.live():
                        bank_free(pe, g, t, position)
                        does[item[0]](e, item[1], bank[item[4]])

            walk(pe, step)

        @block.scalar
        def _(act):
            copy = lambda o, i: nc.scalar.activation(o, i, ACT.Copy)

            def exps(e, k):
                u, part = k // 2, k % 2
                act.wait_ge(done["s"], count("s", e, k))
                if part == 0:
                    wait(act, done["p_lo"], count("p_lo", e.back(2), u))
                nc.scalar.activation(p_f[:, e.off % 2, u, 2 * part:2 * part + 2].rearrange("p h n -> p (h n)"),
                                     in_bank("s", e, k)[:], ACT.Exp).then_inc(done["exp"], 1)

            def p_round(e, u):
                act.wait_ge(done["exp"], count("exp", e, 2 * u + 1))
                before = e.back(2)
                wait(act, done["av"], count("av", before, final("av", before, (u // 2 * 2, u // 2 * 2 + 1))))
                copy(p_hi[:, e.off % 2, u].rearrange("p h n -> p (h n)"),
                     p_f[:, e.off % 2, u].rearrange("p h n -> p (h n)")).then_inc(done["p_hi"], 1)

            def scored(e):
                wait(act, done["s"], count("s", e.back(4), final("s", e.back(4), range(8))))

            def k_round(e, k):
                act.wait_ge(done["k"], count("k", e, k))
                scored(e)
                for odd in range(2):
                    src = in_bank("k", e, k)[odd * D:(odd + 1) * D, :].rearrange("p (j n) -> p j n", j=2)
                    last = copy(k_hl[0:D, e.off % 4, 4 * k + odd:4 * k + 4:2, :], src)
                last.then_inc(done["k_hi"], 1)

            def g_round(e, jt):
                act.wait_ge(done["g"], count("g", e, jt))
                wait(act, done["av"], count("av", e.back(4), final("av", e.back(4), range(4))))
                copy(g_hi[:, e.off % 4, jt, :, 0:D],
                     in_bank("g", e, jt)[:].rearrange("p (h d) -> p h d", h=H)).then_inc(done["g_hi"], 1)

            def max_row_copy(e, k):
                act.wait_ge(done["mt"], count("mt", e))
                scored(e)
                copy(x_lom[D:D + H, e.off % 4, :], in_bank("mt", e)[0:H, 0:N]).then_inc(done["max_row"], 1)

            def c_round(e, k):
                act.wait_ge(ld_c[e.off % 4], e.landed(4, 32))
                for kind in ("k", "g"):
                    wait(act, done[kind], count(kind, e.back(2), final(kind, e.back(2), range(2))))
                copy(c_hi[:, e.off % 2, :], c_in[:, e.off % 4, :]).then_inc(done["c_hi"], 1)

            def x_round(e, k):
                act.wait_ge(done["xn"], count("xn", e))
                scored(e)
                copy(x_hi[:, e.off % 4, :], xn[:, e.off % 2, :]).then_inc(done["x_hi"], 1)

            def xt_round(pr, k):
                act.wait_ge(done["xt"], count("xt", pr))
                wait(act, done["gu"], count("gu", pr.back(1), final("gu", pr, range(3))))
                copy(xt_hi[:].rearrange("p k n -> p (k n)"), in_bank("xt", pr)[:, 0:N]).then_inc(done["xt_hi"], 1)

            def tanh(pr, r):
                act.wait_ge(done["gu"], count("gu", pr, r))
                wait(act, done["gate"], count("gate", pr.back(1), r))
                nc.scalar.activation(th[:, r].rearrange("p k n -> p (k n)"), in_bank("gu", pr, r)[:, 0:2 * P],
                                     ACT.Tanh, scale=0.5 / SC).then_inc(done["tanh"], 1)

            def h_round(pr, r):
                act.wait_ge(done["up"], count("up", pr, r))
                wait(act, done["down"], count("down", pr.back(1)))
                if r < 2:
                    last = copy(h_hi[:, 2 * r:2 * r + 2, :], h_f[:, r])
                else:
                    copy(h_hi[:, 4, :], h_f[:, 2, 0, :])
                    last = copy(h_hi[0:TAIL, 5, :], h_f[0:TAIL, 2, 1, :])
                last.then_inc(done["h_hi"], 1)

            does = {"exp": exps, "p_hi": p_round, "k_hi": k_round, "g_hi": g_round, "max_row": max_row_copy,
                    "c_hi": c_round, "x_hi": x_round, "xt_hi": xt_round, "tanh": tanh, "h_hi": h_round}

            def step(g, t):
                for item in ACT_ORDER:
                    e = work(g, t, item)
                    if e.live():
                        does[item[0]](e, item[1])

            walk(act, step)

        @block.vector
        def _(dve):
            V = nc.vector
            dve.wait_ge(ld_f, 12 * 16)
            for col in (gs_col[:, 0:FT], us_col[:, 0:FT], ts_col[:], ds_col[:]):
                last = V.tensor_scalar(col, col, SC, None, ALU.mult)
            last.then_inc(tail_scaled, 1)
            dve.wait_ge(tail_scaled, 1)
            for k in range(FT):
                V.tensor_scalar(gate_raw[:, k, :], gate_raw[:, k, :], gs_col[:, k:k + 1], None, ALU.mult)
                V.tensor_scalar(up_raw[:, k, :], up_raw[:, k, :], us_col[:, k:k + 1], None, ALU.mult)
            V.tensor_scalar(tail_raw[:], tail_raw[:], ts_col[:], None, ALU.mult)
            for k in range(2):
                last = V.tensor_scalar(down_raw[:, k, :], down_raw[:, k, :], ds_col[:, k:k + 1], None, ALU.mult)
            last.then_inc(tail_scaled, 1)

            n = 0

            def stacked(dst):
                dve.wait_ge(setup_mm, n + 1)
                V.tensor_copy(dst[:], bank[n % 2][:]).then_inc(weights_ready, 1)
                dve.wait_ge(weights_ready, 1 + n // 2)
                V.tensor_tensor(dst[D:P, :], bank[n % 2][D:P, :], dst[D:P, :], ALU.subtract).then_inc(setup_ev, 1)

            stacked(a_w)
            n = 1
            dve.wait_ge(setup_mm, 2)
            V.tensor_copy(woutT[:], bank[1][0:D, :]).then_inc(setup_ev, 1)
            n = 2
            stacked(b_w)
            n = 3
            halves = 2
            for i in range(len(TILES) + FT + 1):
                dve.wait_ge(setup_mm, n + 1)
                if i < len(TILES):
                    m, hi, lo = P, gu_hi[:, :, i, :], gu_lo[:, :, i, :]
                else:
                    k = i - len(TILES)
                    m = P if k < FT else TAIL
                    hi, lo = dn_hi[0:m, k, :].rearrange("p (a n) -> p a n", a=2), dn_lo[0:m, k, :].rearrange(
                        "p (a n) -> p a n", a=2)
                src = bank[n % 2][0:m, 0:N].rearrange("p (a n) -> p a n", a=2)
                V.tensor_copy(hi, src).then_inc(weights_ready, 1)
                halves += 1
                dve.wait_ge(weights_ready, halves)
                V.tensor_tensor(lo, src, hi, ALU.subtract).then_inc(setup_ev, 1)
                n += 1

            def max_reduce(e, k):
                it, hp = k // 4, k % 4
                dve.wait_ge(done["mx"], count("mx", e, k))
                if k == first("max", e):
                    wait(dve, done["mt"], count("mt", e.back(2)))
                V.tensor_reduce(nmax[:, e.off % 2, it, 2 * hp:2 * hp + 2],
                                in_bank("mx", e, k)[:].rearrange("p (h n) -> p h n", h=2), AX_X, ALU.max,
                                negate=True).then_inc(done["max"], 1)

            def weighted(e, k):
                return in_bank("av", e, k)[:, 0:HG * GW].rearrange("p (h d) -> p h d", h=HG)

            def row_sums(e, k):
                dve.wait_ge(done["av"], count("av", e, k))
                V.reciprocal(rsum[:, e.off % 2, k], weighted(e, k)[:, :, D:GW]).then_inc(done["rsum"], 1)

            def normalise(e, k):
                hg, it = k // 2, k % 2
                dve.wait_ge(done["rsum"], count("rsum", e, k))
                if k == first("norm", e):
                    wait(dve, done["sum"], count("sum", e.back(2), 0))
                V.tensor_tensor(heads[:, e.off % 2, hg * HG:(hg + 1) * HG, it, :], weighted(e, k)[:, :, 0:D],
                                rsum[:, e.off % 2, k].to_broadcast([P, HG, D]), ALU.mult).then_inc(done["norm"], 1)

            def k_rest(e, k):
                slot = e.off % 4
                dve.wait_ge(done["k_hi"], count("k_hi", e, k))
                for odd in range(2):
                    src = in_bank("k", e, k)[odd * D:(odd + 1) * D, :].rearrange("p (j n) -> p j n", j=2)
                    hs = slice(4 * k + odd, 4 * k + 4, 2)
                    last = V.tensor_tensor(k_hl[D:P, slot, hs, :], src, k_hl[0:D, slot, hs, :], ALU.subtract)
                last.then_inc(done["k_lo"], 1)

            def k_copy(e, k):
                slot = e.off % 4
                dve.wait_ge(done["k_hi"], count("k_hi", e, final("k_hi", e, range(2))))
                V.tensor_copy(k_hm[0:D, slot].rearrange("p h n -> p (h n)"),
                              k_hl[0:D, slot].rearrange("p h n -> p (h n)")).then_inc(done["k_copy"], 1)

            def g_rest(e, jt):
                slot = e.off % 4
                dve.wait_ge(done["g_hi"], count("g_hi", e, jt))
                V.tensor_tensor(g_lo[:, slot, jt, :, :], in_bank("g", e, jt)[:].rearrange("p (h d) -> p h d", h=H),
                                g_hi[:, slot, jt, :, 0:D], ALU.subtract).then_inc(done["g_lo"], 1)

            def ln_stats(e, k):
                dve.wait_ge(ld_x[e.off % 4], e.landed(4, 32))
                V.bn_stats(stats[:, e.off % 2, :], x_in[:, e.off % 4, :]).then_inc(done["stats"], 1)

            def ln_mean(e, k):
                V.bn_aggr(mv[:, e.off % 2, :], stats[:, e.off % 2, :]).then_inc(done["mean"], 1)

            def ln_eps(e, k):
                dve.wait_ge(done["mean"], count("mean", e))
                V.tensor_scalar(var[:, e.off % 2, :], mv[:, e.off % 2, 1:2], EPS, None, ALU.add).then_inc(done["eps"], 1)

            def ln_apply(e, k):
                dve.wait_ge(done["rstd"], count("rstd", e))
                wait(dve, done["x_lo"], count("x_lo", e.back(2)))
                V.tensor_scalar(xn[:, e.off % 2, :], x_in[:, e.off % 4, :], mv[:, e.off % 2, 0:1], rstd[:, e.off % 2, :],
                                ALU.subtract, ALU.mult).then_inc(done["xn"], 1)

            def residual(pr, k):
                slot = pr.off % 2
                dve.wait_ge(done["yt"], count("yt", pr))
                dve.wait_ge(ld_p[slot], pr.landed(2, 16))
                wait(dve, done["finish"], count("finish", pr.back(2)))
                V.scalar_tensor_tensor(out=x2[:, slot, :], in0=in_bank("yt", pr)[:, 0:N], scalar=bout_col[:],
                                       in1=x_pair[:, slot, :], op0=ALU.add, op1=ALU.add).then_inc(done["x2"], 1)

            def ln2_stats(pr, k):
                dve.wait_ge(done["x2"], count("x2", pr))
                V.bn_stats(stats2[:], x2[:, pr.off % 2, :]).then_inc(done["stats2"], 1)

            def ln2_mean(pr, k):
                V.bn_aggr(mv2[:], stats2[:]).then_inc(done["mean2"], 1)

            def ln2_eps(pr, k):
                dve.wait_ge(done["mean2"], count("mean2", pr))
                V.tensor_scalar(var2[:], mv2[:, 1:2], EPS, None, ALU.add).then_inc(done["eps2"], 1)

            def ln2_apply(pr, k):
                dve.wait_ge(done["rstd2"], count("rstd2", pr))
                wait(dve, done["xt"], count("xt", pr.back(1)))
                V.tensor_scalar(xn2[:], x2[:, pr.off % 2, :], mv2[:, 0:1], rstd2[:], ALU.subtract,
                                ALU.mult).then_inc(done["xn2"], 1)

            def xt_rest(pr, k):
                dve.wait_ge(done["xt_hi"], count("xt_hi", pr))
                V.tensor_tensor(xt_lo[:].rearrange("p k n -> p (k n)"), in_bank("xt", pr)[:, 0:N],
                                xt_hi[:].rearrange("p k n -> p (k n)"), ALU.subtract).then_inc(done["xt_lo"], 1)

            def silu_gate(pr, r):
                dve.wait_ge(done["tanh"], count("tanh", pr, r))
                flat = lambda v: v[:, r].rearrange("p k n -> p (k n)")
                V.scalar_tensor_tensor(out=flat(tg), in0=flat(th), scalar=1.0, in1=in_bank("gu", pr, r)[:, 0:2 * P],
                                       op0=ALU.add, op1=ALU.mult).then_inc(done["gate"], 1)

            def times_up(pr, r):
                b, k = in_bank("gu", pr, r), 0.5 / (SC * SC)
                dve.wait_ge(done["gate"], count("gate", pr, r))
                wait(dve, done["h_lo"], count("h_lo", pr.back(1), r))
                if r < 2:
                    last = V.scalar_tensor_tensor(out=h_f[:, r].rearrange("p k n -> p (k n)"),
                                                  in0=tg[:, r].rearrange("p k n -> p (k n)"), scalar=k,
                                                  in1=b[:, 2 * P:4 * P], op0=ALU.mult, op1=ALU.mult)
                else:
                    V.scalar_tensor_tensor(out=h_f[:, 2, 0, :], in0=tg[:, 2, 0, :], scalar=k, in1=b[:, 2 * P:3 * P],
                                           op0=ALU.mult, op1=ALU.mult)
                    last = V.scalar_tensor_tensor(out=h_f[0:TAIL, 2, 1, :], in0=tg[0:TAIL, 2, 1, :], scalar=k,
                                                  in1=b[TAIL:P, P:2 * P], op0=ALU.mult, op1=ALU.mult)
                last.then_inc(done["up"], 1)

            def finish(pr, k):
                slot = pr.off % 2
                dve.wait_ge(done["down"], count("down", pr))
                wait(dve, st_y[slot], pr.back(2).landed(2, 16))
                V.scalar_tensor_tensor(out=y_out[:, slot, :], in0=in_bank("down", pr)[:, 0:N], scalar=1.0 / SC,
                                       in1=x2[:, slot, :], op0=ALU.mult, op1=ALU.add).then_inc(done["finish"], 1)

            does = {"max": max_reduce, "rsum": row_sums, "norm": normalise, "k_lo": k_rest, "k_copy": k_copy,
                    "g_lo": g_rest, "stats": ln_stats, "mean": ln_mean, "eps": ln_eps, "xn": ln_apply, "x2": residual,
                    "stats2": ln2_stats, "mean2": ln2_mean, "eps2": ln2_eps, "xn2": ln2_apply, "xt_lo": xt_rest,
                    "gate": silu_gate, "up": times_up, "finish": finish}

            STATS_OF = {"mean": "stats", "mean2": "stats2"}

            def step(g, t):
                for position, item in enumerate(DVE_ORDER):
                    nxt = DVE_ORDER[position + 1] if position + 1 < len(DVE_ORDER) else ("", 0, "", 0, -1)
                    if nxt[0] in STATS_OF:
                        assert item[0] != STATS_OF[nxt[0]]
                        e = work(g, t, nxt)
                        if e.live():
                            dve.wait_ge(done[STATS_OF[nxt[0]]], count(STATS_OF[nxt[0]], e))
                    e = work(g, t, item)
                    if e.live():
                        does[item[0]](e, item[1])

            walk(dve, step)

        @block.gpsimd
        def _(pool):
            G = nc.gpsimd
            G.memset(ident[:], 0.0).then_inc(memset_done, 1)
            pool.wait_ge(memset_done, 1)
            G.affine_select(out=ident[:], in_=ident[:], compare_op=ALU.not_equal, fill=1.0, base=0,
                            pattern=[[-1, P]], channel_multiplier=1).then_inc(const_done, 1)
            pool.wait_ge(const_done, 1)
            G.memset(k_hm[D:D + H].rearrange("p s h n -> p (s h n)").bitcast(F32), 0.0).then_inc(memset_done, 1)
            pool.wait_ge(memset_done, 2)
            for slot in range(4):
                v = k_hm[D:D + H, slot]
                last = G.affine_select(out=v, in_=v, compare_op=ALU.not_equal, fill=1.0, base=0,
                                       pattern=[[-1, H], [0, N]], channel_multiplier=1)
            last.then_inc(half_done, 1)
            pool.wait_ge(half_done, 1)
            G.memset(g_hi[:, :, :, :, D:GW], 1.0)
            G.memset(neg_half[:], -0.5).then_inc(half_done, 1)
            pool.wait_ge(half_done, 2)

            def p_rest(e, u):
                pool.wait_ge(done["p_hi"], count("p_hi", e, u))
                row = lambda v: v.rearrange("p h n -> p (h n)")
                G.tensor_tensor(row(p_lo[:, e.off % 2, u]), row(p_f[:, e.off % 2, u]), row(p_hi[:, e.off % 2, u]),
                                ALU.subtract).then_inc(done["p_lo"], 1)

            def head_sum(e, part):
                if part == 0:
                    pool.wait_ge(done["norm"], count("norm", e, final("norm", e, range(4))))
                    o, a, b = half[:, e.off % 2], heads[:, e.off % 2, 0:4], heads[:, e.off % 2, 4:8]
                elif part == 1:
                    pool.wait_ge(done["sum"], count("sum", e, 0))
                    o, a, b = quar[:, e.off % 2], half[:, e.off % 2, 0:2], half[:, e.off % 2, 2:4]
                else:
                    pool.wait_ge(done["sum"], count("sum", e, 1))
                    wait(pool, done["yt"], count("yt", At(e.g, 2, e.off // 2 - 2, NPAIR)))
                    o, a, b = yT[:, e.off // 2 % 2, :, e.off % 2, :], quar[:, e.off % 2, 0], quar[:, e.off % 2, 1]
                G.tensor_tensor(o, a, b, ALU.add).then_inc(done["sum"], 1)

            def x_rest(e, k):
                pool.wait_ge(done["x_hi"], count("x_hi", e))
                G.tensor_tensor(x_lom[0:D, e.off % 4, :], xn[0:D, e.off % 2, :], x_hi[0:D, e.off % 4, :],
                                ALU.subtract).then_inc(done["x_lo"], 1)

            def c_rest(e, k):
                pool.wait_ge(done["c_hi"], count("c_hi", e))
                G.tensor_tensor(c_lo[:, e.off % 2, :], c_in[:, e.off % 4, :], c_hi[:, e.off % 2, :],
                                ALU.subtract).then_inc(done["c_lo"], 1)

            def ln_rstd(e, k):
                pool.wait_ge(done["eps"], count("eps", e))
                G.tensor_tensor(rstd[:, e.off % 2, :], var[:, e.off % 2, :], neg_half[:],
                                ALU.pow).then_inc(done["rstd"], 1)

            def ln2_rstd(pr, k):
                pool.wait_ge(done["eps2"], count("eps2", pr))
                G.tensor_tensor(rstd2[:], var2[:], neg_half[:], ALU.pow).then_inc(done["rstd2"], 1)

            def h_rest(pr, r):
                pool.wait_ge(done["h_hi"], count("h_hi", pr, r))
                if r < 2:
                    last = G.tensor_tensor(h_lo[:, 2 * r:2 * r + 2, :], h_f[:, r], h_hi[:, 2 * r:2 * r + 2, :],
                                           ALU.subtract)
                else:
                    G.tensor_tensor(h_lo[:, 4, :], h_f[:, 2, 0, :], h_hi[:, 4, :], ALU.subtract)
                    last = G.tensor_tensor(h_lo[0:TAIL, 5, :], h_f[0:TAIL, 2, 1, :], h_hi[0:TAIL, 5, :], ALU.subtract)
                last.then_inc(done["h_lo"], 1)

            does = {"p_lo": p_rest, "sum": head_sum, "x_lo": x_rest, "c_lo": c_rest, "rstd": ln_rstd,
                    "rstd2": ln2_rstd, "h_lo": h_rest}

            def step(g, t):
                for item in POOL_ORDER:
                    e = work(g, t, item)
                    if e.live():
                        does[item[0]](e, item[1])

            walk(pool, step)


_INS = ["x", "ctx_2048", "L0_xattn_Wq", "L0_xattn_Wkv", "L0_xattn_Wout", "L0_xattn_bout", "L0_ffn_gate_w",
        "L0_ffn_up_w", "L0_ffn_down_w", "L0_ffn_gate_s", "L0_ffn_up_s", "L0_ffn_down_s"]


def kernel(**inputs):
    import numpy as _np
    import concourse.bacc as _bacc
    from concourse import mybir as _mybir
    from concourse.bass_utils import run_bass_kernel_spmd as _run

    nc = _bacc.Bacc("TRN2", target_bir_lowering=False, num_devices=1)
    arrays, args = {}, []
    for name in _INS:
        a = _np.ascontiguousarray(inputs[name])
        arrays[f"in_{name}_dram"] = a
        args.append(nc.dram_tensor(f"in_{name}_dram", a.shape, _mybir.dt.from_np(a.dtype), kind="ExternalInput").ap())
    dt = _mybir.dt.from_np(_np.dtype("float32"))
    args.append(nc.dram_tensor("out_dram", inputs["x"].shape, dt, kind="ExternalOutput").ap())
    xattn_ffn(nc, *args)
    r = _run(nc, [arrays], core_ids=[0])
    return r.results[0]["out_dram"]
```

```python
from contextlib import ExitStack

import concourse.bass as bass
from concourse import mybir

ALU = mybir.AluOpType
ACT = mybir.ActivationFunctionType
F32 = mybir.dt.float32
F16 = mybir.dt.float16
AX_X = mybir.AxisListType.X

P = 128
EPS = 1e-5
SC = 16.0
BODY = 4
B_PRODUCTS_AT = 7
B_SPLIT_AT = (0, 26)
SCALE_WEIGHTS_AT = (0, 55)


def orders(text):
    items = []
    for token in text.split():
        name, place = token.split("@")
        kind, _, what = name.partition(":")
        lag, _, bank = place.partition("/")
        part = what.rstrip("ab")
        items.append((kind, int(part or 0), what[len(part):], int(lag), int(bank or -1)))
    return items


PE_ORDER = orders("""
    xt@5/3 k:1a@0/4 k:0a@0/5 s:2a@1/6 s:3a@1/7 mx:5b@1/0 k:0b@0/1 mx:6b@1/4 s:4a@1/6 av:0b@2/2 down@6/0 yt@4/4
    s:5a@1/7 mx:7b@1/3 av:2a@2/5 av:3a@2/0 s:6a@1/6 mt:b@1/1 av:1b@2/3 k:1b@0/4 g:0a@0/5 mx:0a@0/0 s:7a@1/7
    g:1a@0/2 s:0b@1/6 mx:1a@0/0 mx:2a@0/3 av:2b@2/1 s:1b@1/7 mx:3a@0/5 s:2b@1/6 mx:4a@0/3 av:3b@2/4 mx:0b@0/2
    s:3b@1/7 s:4b@1/6 mx:5a@0/1 mx:6a@0/0 mx:7a@0/4 gu:0@5/5 s:5b@1/7 mx:1b@0/1 mx:2b@0/3 g:1b@0/4 mx:3b@0/0
    s:6b@1/6 mt:a@0/3 gu:1@5/2 g:0b@0/5 s:7b@1/7 mx:4b@0/3 s:0a@0/6 gu:2@5/1 av:0a@1/0 s:1a@0/7 av:1a@1/2
""")
ACT_ORDER = orders("""
    c_hi:a@0 exp:6b@2 max_row:a@1 tanh:1@6 c_hi:b@0 g_hi:0b@1 exp:7b@2 h_hi:0@6 exp:0a@1 tanh:2@6 p_hi:2b@2
    h_hi:1@6 exp:1a@1 h_hi:2@6 k_hi:1a@0 k_hi:0a@0 exp:2a@1 p_hi:3b@2 exp:3a@1 xt_hi@5 p_hi:0a@1 exp:4a@1
    k_hi:0b@0 p_hi:1a@1 exp:5a@1 exp:6a@1 x_hi:a@0 max_row:b@1 p_hi:2a@1 g_hi:0a@0 k_hi:1b@0 exp:7a@1 exp:0b@1
    g_hi:1a@0 x_hi:b@0 exp:1b@1 exp:2b@1 p_hi:0b@1 exp:3b@1 exp:4b@1 p_hi:3a@1 exp:5b@1 tanh:0@5 p_hi:1b@1
    g_hi:1b@0
""")
DVE_ORDER = orders("""
    stats:a@0 up:1@6 stats:b@0 g_lo:0b@1 mean:a@0 max:4b@1 mean:b@0 gate:2@6 eps:a@0 rsum:0a@2 up:2@6 norm:0a@2
    rsum:1a@2 eps:b@0 h_lo:0@6 norm:1a@2 k_lo:1a@0 h_lo:1@6 max:5b@1 h_lo:2@6 max:6b@1 k_lo:0a@0 xt_lo@5
    rsum:0b@2 finish@6 xn:a@0 x2@4 max:7b@1 k_lo:0b@0 rsum:2a@2 stats2@4 rsum:3a@2 mean2@4 norm:2a@2 norm:3a@2
    rsum:1b@2 norm:1b@2 norm:0b@2 xn:b@0 max:0a@0 g_lo:0a@0 k_lo:1b@0 max:2a@0 rsum:2b@2 g_lo:1a@0 eps2@4
    max:3a@0 max:1a@0 rsum:3b@2 norm:2b@2 norm:3b@2 max:4a@0 max:5a@0 max:7a@0 max:6a@0 max:0b@0 max:2b@0
    gate:0@5 max:3b@0 up:0@5 max:1b@0 xn2@4 g_lo:1b@0 gate:1@5
""")
POOL_ORDER = orders("""
    p_lo:3a@2 c_lo:a@0 sum:2a@3 c_lo:b@0 p_lo:1b@2 sum:0b@3 rstd:a@0 sum:1b@3 p_lo:2b@2 rstd:b@0 sum:2b@3
    p_lo:3b@2 p_lo:0a@1 p_lo:1a@1 sum:0a@2 p_lo:2a@1 rstd2@4 sum:1a@2 x_lo:a@0 x_lo:b@0 p_lo:0b@1
""")
SP_ORDER = orders("""
    load_c:a@0 load_x:a@0 move_lo:a@1 load_c:b@0 move_lo:b@1 load_x:b@0 move_hi:b@1 store@6 load_pair@2
    move_hi:a@0
""")

ALL_ORDERS = (PE_ORDER, ACT_ORDER, DVE_ORDER, POOL_ORDER, SP_ORDER)


class At:

    def __init__(self, g, per, off, total):
        self.g, self.per, self.off, self.total = g, per, off, total

    def live(self):
        return not isinstance(self.g, int) or 0 <= self.per * self.g + self.off < self.total

    def back(self, k):
        return At(self.g, self.per, self.off - k, self.total)

    def landed(self, slots, inc):
        if isinstance(self.g, int):
            return ((self.per * self.g + self.off) // slots + 1) * inc
        return self.g * (self.per // slots * inc) + (self.off // slots + 1) * inc


def wait(eng, sem, value):
    if not isinstance(value, int) or value > 0:
        eng.wait_ge(sem, value)


def xattn_ffn(nc, x, ctx_in, wq, wkv, wout, bout, gate_w, up_w, down_w, gate_s, up_s, down_s, out):
    NB, C, N = x.shape
    HID = wq.shape[0]
    D = 64
    H = HID // D
    INTER = gate_w.shape[0]
    NPAIR = NB // 2
    IT = N // P
    FT = INTER // P
    TAIL = INTER - FT * P
    assert C == D == 64 and N == 256 and H == 8 and FT == 5 and TAIL == 64
    HC = H * D
    GW = D + 1
    HG = H // 2
    ROUNDS = [["g0", "g1", "u0", "u1"], ["g2", "g3", "u2", "u3"], ["g4", "t", "u4"]]
    TILES = [name for r in ROUNDS for name in r]

    with ExitStack() as stack:
        def sb(name, shape, dt=F32):
            return stack.enter_context(nc.sbuf_tensor(name, shape, dt))

        def psum(name, shape):
            return stack.enter_context(nc.psum_tensor(name, shape, F32))

        def sem(name):
            return stack.enter_context(nc.semaphore(name))

        ident = sb("ident", [P, P])
        neg_half = sb("neg_half", [P, 1])
        gs_col = sb("gs_col", [P, FT + 1])
        us_col = sb("us_col", [P, FT + 1])
        ts_col = sb("ts_col", [P, 1])
        ds_col = sb("ds_col", [P, 2])
        bout_col = sb("bout_col", [P, 1])
        a_w = sb("a_w", [P, HC], F16)
        b_w = sb("b_w", [P, HC], F16)
        gu_hi = sb("gu_hi", [P, 2, len(TILES), P], F16)
        gu_lo = sb("gu_lo", [P, 2, len(TILES), P], F16)
        dn_hi = sb("dn_hi", [P, FT + 1, N], F16)
        dn_lo = sb("dn_lo", [P, FT + 1, N], F16)
        x_in = sb("x_in", [P, 4, N])
        c_in = sb("c_in", [P, 4, N])
        c_hi = sb("c_hi", [P, 2, N], F16)
        c_lo = sb("c_lo", [P, 2, N], F16)
        stats = sb("stats", [P, 2, 6])
        mv = sb("mv", [P, 2, 2])
        var = sb("var", [P, 2, 1])
        rstd = sb("rstd", [P, 2, 1])
        xn = sb("xn", [P, 2, N])
        x_hi = sb("x_hi", [P, 4, N], F16)
        x_lom = sb("x_lom", [P, 4, N], F16)
        kk_hi = sb("kk_hi", [P, 4, H // 2, N], F16)
        kk_lo = sb("kk_lo", [P, 2, H // 2, N], F16)
        k_hl = sb("k_hl", [P, 4, 2, H // 2, N], F16)
        k_hm = sb("k_hm", [P, 4, 2, H // 2, N], F16)
        g_hi = sb("g_hi", [P, 4, IT, H, GW], F16)
        g_lo = sb("g_lo", [P, 4, IT, H, D], F16)
        nmax = sb("nmax", [P, 2, IT, H])
        p_f = sb("p_f", [P, 2, 4, HG, N])
        p_hi = sb("p_hi", [P, 2, 4, HG, N], F16)
        p_lo = sb("p_lo", [P, 2, 4, HG, N], F16)
        def region(whole, m):
            at = 0

            def part(*shape, dt=F32):
                nonlocal at
                words = 1
                for n in shape:
                    words *= n
                words = words * 2 // 4 if dt == F16 else words
                names = " ".join(f"d{i}" for i in range(len(shape)))
                flat = whole[0:m, at:at + words]
                at += words
                assert at <= whole.shape[1]
                return (flat.bitcast(F16) if dt == F16 else flat).rearrange(
                    f"p ({names}) -> p {names}", **{f"d{i}": n for i, n in enumerate(shape)})

            return part

        raw = region(p_f[:].rearrange("p e u h n -> p (e u h n)"), D)
        wk2, wv2 = raw(H, 2, D), raw(H, 2, D)
        wq_sb, wout_sb, woutT = raw(H, D), raw(HC), raw(HC)
        rsum = sb("rsum", [P, 2, 4, HG, 1])
        heads = sb("heads", [P, 2, H, IT, D])
        x_pair = sb("x_pair", [P, 2, N])
        late = sb("late", [P, 19 * N])
        view = region(late, P)
        yT = view(2, IT, 2, D)
        x2 = view(2, N)
        xn2 = view(N)
        th, tg, h_f = (view(3, 2, P) for _ in range(3))
        h_hi, h_lo = (view(FT + 1, P, dt=F16) for _ in range(2))
        y_out = view(2, N)
        raw = region(late, P)
        gate_raw, tail_raw, up_raw, down_raw = raw(FT, N), raw(N), raw(FT, N), raw(2, INTER)
        stats2 = sb("stats2", [P, 6])
        mv2 = sb("mv2", [P, 2])
        var2 = sb("var2", [P, 1])
        rstd2 = sb("rstd2", [P, 1])
        xt_hi = sb("xt_hi", [P, 2, P], F16)
        xt_lo = sb("xt_lo", [P, 2, P], F16)

        bank = [psum(f"bank{i}", [P, 512]) for i in range(8)]


        ld_a, ld_b, ld_f = sem("ld_a"), sem("ld_b"), sem("ld_f")
        ld_x = [sem(f"ld_x{i}") for i in range(4)]
        ld_c = [sem(f"ld_c{i}") for i in range(4)]
        mv_k = [sem(f"mv_k{i}") for i in range(4)]
        ld_p = [sem(f"ld_p{i}") for i in range(2)]
        st_y = [sem(f"st_y{i}") for i in range(2)]
        memset_done, const_done, ones_done = sem("memset_done"), sem("const_done"), sem("ones_done")
        setup_mm, setup_ev = sem("setup_mm"), sem("setup_ev")
        scaled = sem("scaled")
        weights_ready = sem("weights_ready")
        ffn_set = [sem(f"ffn_set{n}") for n in range(10)]
        done = {kind: sem(f"{kind}_done") for order in ALL_ORDERS[:4]
                for kind in sorted({item[0] for item in order})}

        PLACES = {}
        for order in ALL_ORDERS:
            for position, (kind, k, who, lag, _) in enumerate(order):
                PLACES.setdefault(kind, {})[k, who] = (lag, position)
        BANK = {(kind, k, who): number for kind, k, who, _, number in PE_ORDER}

        def whose(e):
            return "" if e.per == 2 else "ab"[e.off % 2]

        def period(e):
            return e.off if e.per == 2 else e.off // 2

        def count(kind, e, k=0):
            places = PLACES[kind]
            lag, position = places[k, whose(e)]
            ahead = [period(e) + lag - other - (after > position) + 1 for other, after in places.values()]

            def at(g):
                return sum(min(max(2 * g + n, 0), NPAIR) for n in ahead)

            if isinstance(e.g, int):
                return at(e.g) if 2 * e.g + period(e) >= 0 else 0
            steady = sum(ahead)
            for g in (FIRST_FULL, LAST_FULL - 1):
                assert 2 * g + period(e) >= 0 and at(g) == 2 * len(ahead) * g + steady, (kind, k)
            return e.g * (2 * len(ahead)) + steady

        def final(kind, e, parts):
            return max(parts, key=lambda k: PLACES[kind][k, whose(e)])

        def first(kind, e):
            return min((k for k, who in PLACES[kind] if who == whose(e)), key=lambda k: PLACES[kind][k, whose(e)])

        assert len(TILES) == 11
        FFN_GROUPS = [("gu", 0, 2), ("gu", 4, 6), ("gu", 8, 10), ("gu", 2, 4), ("gu", 6, 8), ("gu", 10, 11),
                      ("dn", 0, 2), ("dn", 2, 4), ("dn", 4, 5), ("dn", 5, 6)]

        def weights_group(e, r):
            if e.per != 2 or not isinstance(e.g, int) or 2 * e.g + e.off >= 0:
                return None
            n = (2 * e.g + e.off + 4) * 3 + r
            return n if 0 <= n < len(FFN_GROUPS) else None

        def group_views(n, r):
            what, first_k, end_k = FFN_GROUPS[n]
            m = TAIL if (what, first_k) == ("dn", FT) else P
            src = bank[BANK["gu", r, ""]][0:m, 0:(end_k - first_k) * N]
            if what == "gu":
                return (src.rearrange("p (k w n) -> p k w n", k=2, n=P), gu_hi[:, :, first_k:end_k, :],
                        gu_lo[:, :, first_k:end_k, :])
            return src.rearrange("p (w n) -> p w n", n=N), dn_hi[0:m, first_k:end_k, :], dn_lo[0:m, first_k:end_k, :]

        def in_bank(kind, e, k=0):
            return bank[BANK[kind, k, whose(e)]]

        def work(g, t, item):
            _, _, who, lag, _ = item
            if who:
                return At(g, 4, 2 * (t - lag) + "ab".index(who), NB)
            return At(g, 2, t - lag, NPAIR)

        READER = {"mx": "max", "av": "norm", "k": "k_lo", "g": "g_lo", "mt": "max_row", "yt": "x2", "xt": "xt_lo",
                  "gu": "up", "down": "finish", "s": "exp"}

        def bank_free(pe, g, t, position):
            number, before = PE_ORDER[position][4], position
            while True:
                before -= 1
                if before < 0:
                    before += len(PE_ORDER)
                    t -= 1
                if isinstance(g, int) and 2 * g + t < 0:
                    return
                kind, k, _, _, other = PE_ORDER[before]
                e = work(g, t, PE_ORDER[before])
                if other == number and e.live():
                    wait(pe, done[READER[kind]], count(READER[kind], e, k))
                    return
                if other == number and kind == "gu" and weights_group(e, k) is not None:
                    pe.wait_ge(ffn_set[weights_group(e, k)], 3)
                    return

        K_MOVES = 6 * 16

        block = stack.enter_context(nc.Block())

        LAG_END = max(item[3] for order in ALL_ORDERS for item in order)
        GROUPS = (NPAIR + LAG_END + 1) // 2
        FIRST_FULL = 5
        LAST_FULL = NPAIR // 2

        def walk(eng, step, last_full=LAST_FULL):
            for g in range(FIRST_FULL):
                for t in range(2):
                    step(g, t)
            with eng.Fori(FIRST_FULL, last_full) as g:
                for t in range(2):
                    step(g, t)
            for g in range(last_full, GROUPS):
                for t in range(2):
                    step(g, t)

        @block.sync
        def _(sp):
            kv = wkv.rearrange("(s h d) c -> s d h c", s=2, d=D)
            sp.dma_start(wq_sb, wq.rearrange("(h d) c -> d h c", d=D)).then_inc(ld_a, 16)
            for c in range(2):
                sp.dma_start(wk2[:, :, c, :], kv[0]).then_inc(ld_a, 16)

            def load(e, dst, src, into, used):
                wait(sp, done[used], count(used, e.back(4)))
                for lo in (0, D):
                    sp.dma_start(dst[lo:lo + D, e.off % 4, :], src[bass.ds(e.g * BODY + e.off, 1)].rearrange(
                        "b c n -> (b c) n")).then_inc(into[e.off % 4], 16)

            def load_x(e, k):
                load(e, x_in, x, ld_x, "xn")

            def load_c(e, k):
                load(e, c_in, ctx_in, ld_c, "c_lo")

            def load_pair(pr, k):
                slot = pr.off % 2
                wait(sp, done["x2"], count("x2", pr.back(2)))
                sp.dma_start(x_pair[:, slot, :], x[bass.ds(pr.g * BODY + 2 * pr.off, 2)].rearrange(
                    "b c n -> (b c) n")).then_inc(ld_p[slot], 16)

            def store(pr, k):
                slot = pr.off % 2
                sp.wait_ge(done["finish"], count("finish", pr))
                sp.dma_start(out[bass.ds(pr.g * BODY + 2 * pr.off, 2)].rearrange("b c n -> (b c) n"),
                             y_out[:, slot, :]).then_inc(st_y[slot], 16)

            def move_hi(e, k):
                slot = e.off % 4
                sp.wait_ge(done["k_hi"], count("k_hi", e, final("k_hi", e, range(2))))
                for odd in range(2):
                    for dst in (k_hl, k_hm):
                        sp.dma_start(dst[0:D, slot, odd], kk_hi[odd * D:(odd + 1) * D, slot]).then_inc(mv_k[slot], 16)

            def move_lo(e, k):
                slot = e.off % 4
                sp.wait_ge(done["k_lo"], count("k_lo", e, final("k_lo", e, range(2))))
                for odd in range(2):
                    sp.dma_start(k_hl[D:P, slot, odd], kk_lo[odd * D:(odd + 1) * D, e.off % 2]).then_inc(mv_k[slot], 16)

            does = {"load_x": load_x, "load_c": load_c, "load_pair": load_pair, "store": store, "move_hi": move_hi,
                    "move_lo": move_lo}

            def step(g, t):
                for item in SP_ORDER:
                    e = work(g, t, item)
                    loaded = item[2] and item[0] in ("load_x", "load_c") and isinstance(e.g, int) and 4 * e.g + e.off < 2
                    if e.live() and not loaded:
                        does[item[0]](e, item[1])

            load_c(At(0, BODY, 0, NB), 0)
            load_x(At(0, BODY, 0, NB), 0)
            sp.dma_start(wout_sb, wout).then_inc(ld_b, 16)
            for c in range(2):
                sp.dma_start(wv2[:, :, c, :], kv[1]).then_inc(ld_b, 16)
            load_c(At(0, BODY, 1, NB), 0)
            load_x(At(0, BODY, 1, NB), 0)
            for n, w_ap, raw, s_ap, col in ((0, gate_w, gate_raw, gate_s, gs_col), (1, up_w, up_raw, up_s, us_col)):
                sp.dma_start(raw[:, 0:FT, :], w_ap[0:FT * P].rearrange("(k p) n -> p k n", p=P)).then_inc(ld_f, 16)
                sp.dma_start(tail_raw[n * TAIL:(n + 1) * TAIL, :], w_ap[FT * P:INTER]).then_inc(ld_f, 16)
                sp.dma_start(col[:, 0:FT], s_ap[0:FT * P].rearrange("(k p) -> p k", p=P),
                             allow_slow_non_contiguous=True).then_inc(ld_f, 16)
                sp.dma_start(ts_col[n * TAIL:(n + 1) * TAIL, :],
                             s_ap[FT * P:INTER].rearrange("(p a) -> p a", a=1)).then_inc(ld_f, 16)
            sp.dma_start(down_raw[:], down_w.rearrange("(k p) i -> p k i", p=P)).then_inc(ld_f, 16)
            sp.dma_start(ds_col[:], down_s.rearrange("(k p) -> p k", p=P),
                         allow_slow_non_contiguous=True).then_inc(ld_f, 16)
            for n in range(2):
                sp.dma_start(bout_col[n * D:(n + 1) * D, :], bout.rearrange("(p a) -> p a", a=1)).then_inc(ld_f, 16)
            walk(sp, step)
            for slot in range(2):
                sp.wait_ge(st_y[slot], NPAIR // 2 * 16)

        @block.tensor
        def _(pe):
            mm = nc.tensor.matmul
            pe.wait_ge(ld_a, 3 * 16)
            for h in range(H):
                last = mm(bank[6][:, h * D:(h + 1) * D], wk2[:, h].rearrange("d a c -> d (a c)"), wq_sb[:, h, :],
                          start=True, stop=True)
            last.then_inc(setup_mm, 1)
            pe.wait_ge(ld_b, 3 * 16)
            pe.wait_ge(const_done, 1)
            for h in range(H):
                last = nc.tensor.transpose(bank[7][0:D, h * D:(h + 1) * D], wout_sb[:, h * D:(h + 1) * D],
                                           ident[0:D, 0:D])
            last.then_inc(setup_mm, 1)
            pe.wait_ge(setup_ev, 1)

            def b_products():
                pe.wait_ge(setup_ev, 2)
                for h in range(H):
                    last = mm(bank[6][:, h * D:(h + 1) * D], wv2[:, h].rearrange("d a c -> d (a c)"),
                              woutT[:, h * D:(h + 1) * D], start=True, stop=True)
                last.then_inc(setup_mm, 1)

            def constants():
                pe.wait_ge(setup_ev, 3)
                pe.wait_ge(ones_done, 2)
                pe.wait_ge(memset_done, 2)

            def ffn_weights(n, dst):
                pe.wait_ge(scaled, 2)
                what, first_k, end_k = FFN_GROUPS[n]
                for i in range(first_k, end_k):
                    for k in range(2):
                        if what == "gu":
                            src = tail_raw if TILES[i] == "t" else {"g": gate_raw, "u": up_raw}[TILES[i][0]][
                                :, int(TILES[i][1]), :]
                            m, src, col = P, src[:, k * P:(k + 1) * P], (k * (end_k - first_k) + i - first_k) * P
                        else:
                            m = P if i < FT else TAIL
                            src, col = down_raw[:, k, i * P:i * P + m], (i - first_k) * N + k * P
                        last = nc.tensor.transpose(dst[0:m, col:col + P], src, ident[:])
                last.then_inc(ffn_set[n], 1)

            def scores(e, k, dst):
                slot, hg, jt = e.off % 4, k // 4, k // 2 % 2
                if k == first("s", e):
                    pe.wait_ge(done["x_lo"], count("x_lo", e))
                    pe.wait_ge(done["max_row"], count("max_row", e))
                    pe.wait_ge(mv_k[slot], e.landed(4, K_MOVES))
                for i in range(2):
                    h = hg * HG + k % 2 * 2 + i
                    col = slice(i * N, (i + 1) * N)
                    mm(dst[:, col], k_hl[:, slot, h % 2, h // 2, jt * P:(jt + 1) * P], x_hi[:, slot, :], start=True, stop=False)
                    last = mm(dst[:, col], k_hm[0:D + H, slot, h % 2, h // 2, jt * P:(jt + 1) * P], x_lom[0:D + H, slot, :],
                              start=False, stop=True)
                last.then_inc(done["s"], 1)

            def maxima(e, k, dst):
                slot, it, hp, odd = e.off % 4, k // 4, k % 4 // 2, k % 2
                rows = slice(odd * D, (odd + 1) * D)
                pe.wait_ge(done["x_hi"], count("x_hi", e))
                pe.wait_ge(done["k_hi"], count("k_hi", e, hp))
                mm(dst[:], x_hi[rows, slot, it * P:(it + 1) * P],
                   kk_hi[rows, slot, 2 * hp:2 * hp + 2, :].rearrange("p h n -> p (h n)"),
                   start=True, stop=True).then_inc(done["mx"], 1)

            def attend(e, k, dst):
                slot, hg, it = e.off % 4, k // 2, k % 2
                pe.wait_ge(done["p_lo"], count("p_lo", e, final("p_lo", e, (2 * hg, 2 * hg + 1))))
                if k == first("av", e):
                    pe.wait_ge(done["g_lo"], count("g_lo", e, final("g_lo", e, range(2))))
                for i in range(HG):
                    o = dst[:, i * GW:(i + 1) * GW]
                    for jt in range(IT):
                        ph = p_hi[:, e.off % 2, 2 * hg + jt, i, it * P:(it + 1) * P]
                        pl = p_lo[:, e.off % 2, 2 * hg + jt, i, it * P:(it + 1) * P]
                        gh = g_hi[:, slot, jt, hg * HG + i, :]
                        gl = g_lo[:, slot, jt, hg * HG + i, :]
                        mm(o, ph, gh, start=jt == 0, stop=False)
                        mm(o[:, 0:D], ph, gl, start=False, stop=False)
                        last = mm(o, pl, gh, start=False, stop=jt == IT - 1)
                last.then_inc(done["av"], 1)

            def keys(e, k, dst):
                slot = e.off % 2
                pe.wait_ge(done["c_lo"], count("c_lo", e))
                for j in range(2):
                    o, w = dst[:, j * N:(j + 1) * N], a_w[:, (2 * k + j) * P:(2 * k + j + 1) * P]
                    mm(o, w, c_hi[:, slot, :], start=True, stop=False)
                    last = mm(o, w, c_lo[:, slot, :], start=False, stop=True)
                last.then_inc(done["k"], 1)

            def values(e, jt, dst):
                slot = e.off % 2
                pe.wait_ge(done["c_lo"], count("c_lo", e))
                mm(dst[:], c_hi[:, slot, jt * P:(jt + 1) * P], b_w[:], start=True, stop=False)
                mm(dst[:], c_lo[:, slot, jt * P:(jt + 1) * P], b_w[:], start=False, stop=True).then_inc(done["g"], 1)

            def max_rows(e, k, dst):
                pe.wait_ge(done["max"], count("max", e, final("max", e, range(8))))
                for it in range(IT):
                    last = nc.tensor.transpose(dst[0:H, it * P:(it + 1) * P], nmax[:, e.off % 2, it, :], ident[:])
                last.then_inc(done["mt"], 1)

            def y_rows(pr, k, dst):
                for odd in range(2):
                    pe.wait_ge(done["sum"], count("sum", At(pr.g, 4, 2 * pr.off + odd, NB), 2))
                for it in range(IT):
                    last = nc.tensor.transpose(dst[:, it * P:(it + 1) * P],
                                               yT[:, pr.off % 2, it].rearrange("p b c -> p (b c)"), ident[:])
                last.then_inc(done["yt"], 1)

            def xn2_cols(pr, k, dst):
                pe.wait_ge(done["xn2"], count("xn2", pr))
                for j in range(2):
                    last = nc.tensor.transpose(dst[:, j * P:(j + 1) * P], xn2[:, j * P:(j + 1) * P], ident[:])
                last.then_inc(done["xt"], 1)

            def gate_up(pr, r, dst):
                if isinstance(pr.g, int) and 2 * pr.g + pr.off == 0:
                    for group in ffn_set:
                        pe.wait_ge(group, 3)
                pe.wait_ge(done["xt_lo"], count("xt_lo", pr))
                for i, name in enumerate(ROUNDS[r]):
                    w, o = TILES.index(name), dst[:, i * P:(i + 1) * P]
                    passes = [(a, b, j) for j in range(2) for a, b in ((gu_hi, xt_hi), (gu_lo, xt_hi), (gu_hi, xt_lo))]
                    for n, (a, b, j) in enumerate(passes):
                        last = mm(o, a[:, j, w, :], b[:, j, :], start=n == 0, stop=n == len(passes) - 1)
                last.then_inc(done["gu"], 1)

            def down(pr, k, dst):
                pe.wait_ge(done["h_lo"], count("h_lo", pr, final("h_lo", pr, range(3))))
                passes = [(a, b, j) for j in range(FT + 1) for a, b in ((h_hi, dn_hi), (h_lo, dn_hi), (h_hi, dn_lo))]
                for n, (a, b, j) in enumerate(passes):
                    m = P if j < FT else TAIL
                    last = mm(dst[:, 0:N], a[0:m, j, :], b[0:m, j, :], start=n == 0, stop=n == len(passes) - 1)
                last.then_inc(done["down"], 1)

            does = {"s": scores, "mx": maxima, "av": attend, "k": keys, "g": values, "mt": max_rows, "yt": y_rows,
                    "xt": xn2_cols, "gu": gate_up, "down": down}

            def step(g, t):
                for position, item in enumerate(PE_ORDER):
                    if isinstance(g, int) and 2 * g + t == 0:
                        if position == B_PRODUCTS_AT:
                            b_products()
                        if item[0] == "g" and all(before[0] != "g" for before in PE_ORDER[:position]):
                            constants()
                    e = work(g, t, item)
                    group = weights_group(e, item[1]) if item[0] == "gu" else None
                    if group is not None:
                        bank_free(pe, g, t, position)
                        ffn_weights(group, bank[item[4]])
                    if e.live():
                        bank_free(pe, g, t, position)
                        does[item[0]](e, item[1], bank[item[4]])

            walk(pe, step)

        @block.scalar
        def _(act):
            copy = lambda o, i: nc.scalar.activation(o, i, ACT.Copy)

            def head_ones(slot):
                for odd in range(2):
                    diag = ident[D:D + H, D + odd:D + H:2].unsqueeze(2).to_broadcast([H, H // 2, N])
                    last = copy(k_hm[D:D + H, slot, odd], diag)
                return last

            act.wait_ge(const_done, 1)
            head_ones(0)
            head_ones(1).then_inc(ones_done, 1)

            def ffn_hi(n, r):
                act.wait_ge(ffn_set[n], 1)
                src, hi, _ = group_views(n, r)
                copy(hi, src).then_inc(ffn_set[n], 1)

            def exps(e, k):
                u, part = k // 2, k % 2
                act.wait_ge(done["s"], count("s", e, k))
                if part == 0:
                    wait(act, done["p_lo"], count("p_lo", e.back(2), u))
                nc.scalar.activation(p_f[:, e.off % 2, u, 2 * part:2 * part + 2].rearrange("p h n -> p (h n)"),
                                     in_bank("s", e, k)[:], ACT.Exp).then_inc(done["exp"], 1)

            def p_round(e, u):
                act.wait_ge(done["exp"], count("exp", e, 2 * u + 1))
                before = e.back(2)
                wait(act, done["av"], count("av", before, final("av", before, (u // 2 * 2, u // 2 * 2 + 1))))
                copy(p_hi[:, e.off % 2, u].rearrange("p h n -> p (h n)"),
                     p_f[:, e.off % 2, u].rearrange("p h n -> p (h n)")).then_inc(done["p_hi"], 1)

            def scored(e):
                wait(act, done["s"], count("s", e.back(4), final("s", e.back(4), range(8))))

            def k_round(e, k):
                act.wait_ge(done["k"], count("k", e, k))
                scored(e)
                copy(kk_hi[:, e.off % 4, 2 * k:2 * k + 2, :],
                     in_bank("k", e, k)[:].rearrange("p (j n) -> p j n", j=2)).then_inc(done["k_hi"], 1)

            def g_round(e, jt):
                act.wait_ge(done["g"], count("g", e, jt))
                wait(act, done["av"], count("av", e.back(4), final("av", e.back(4), range(4))))
                copy(g_hi[:, e.off % 4, jt, :, 0:D],
                     in_bank("g", e, jt)[:].rearrange("p (h d) -> p h d", h=H)).then_inc(done["g_hi"], 1)

            def max_row_copy(e, k):
                act.wait_ge(done["mt"], count("mt", e))
                scored(e)
                copy(x_lom[D:D + H, e.off % 4, :], in_bank("mt", e)[0:H, 0:N]).then_inc(done["max_row"], 1)

            def c_round(e, k):
                act.wait_ge(ld_c[e.off % 4], e.landed(4, 32))
                for kind in ("k", "g"):
                    wait(act, done[kind], count(kind, e.back(2), final(kind, e.back(2), range(2))))
                copy(c_hi[:, e.off % 2, :], c_in[:, e.off % 4, :]).then_inc(done["c_hi"], 1)

            def x_round(e, k):
                act.wait_ge(done["xn"], count("xn", e))
                scored(e)
                copy(x_hi[:, e.off % 4, :], xn[:, e.off % 2, :]).then_inc(done["x_hi"], 1)

            def xt_round(pr, k):
                act.wait_ge(done["xt"], count("xt", pr))
                wait(act, done["gu"], count("gu", pr.back(1), final("gu", pr, range(3))))
                copy(xt_hi[:].rearrange("p k n -> p (k n)"), in_bank("xt", pr)[:, 0:N]).then_inc(done["xt_hi"], 1)

            def tanh(pr, r):
                act.wait_ge(done["gu"], count("gu", pr, r))
                wait(act, done["gate"], count("gate", pr.back(1), r))
                nc.scalar.activation(th[:, r].rearrange("p k n -> p (k n)"), in_bank("gu", pr, r)[:, 0:2 * P],
                                     ACT.Tanh, scale=0.5 / SC).then_inc(done["tanh"], 1)

            def h_round(pr, r):
                act.wait_ge(done["up"], count("up", pr, r))
                wait(act, done["down"], count("down", pr.back(1)))
                if r < 2:
                    last = copy(h_hi[:, 2 * r:2 * r + 2, :], h_f[:, r])
                else:
                    copy(h_hi[:, 4, :], h_f[:, 2, 0, :])
                    last = copy(h_hi[0:TAIL, 5, :], h_f[0:TAIL, 2, 1, :])
                last.then_inc(done["h_hi"], 1)

            does = {"exp": exps, "p_hi": p_round, "k_hi": k_round, "g_hi": g_round, "max_row": max_row_copy,
                    "c_hi": c_round, "x_hi": x_round, "xt_hi": xt_round, "tanh": tanh, "h_hi": h_round}

            def step(g, t):
                for item in ACT_ORDER:
                    e = work(g, t, item)
                    if item[0] == "tanh" and weights_group(e, item[1]) is not None:
                        ffn_hi(weights_group(e, item[1]), item[1])
                    if e.live():
                        does[item[0]](e, item[1])

            walk(act, step)

        @block.vector
        def _(dve):
            V = nc.vector
            def head_ones(slot):
                for odd in range(2):
                    diag = ident[D:D + H, D + odd:D + H:2].unsqueeze(2).to_broadcast([H, H // 2, N])
                    last = V.tensor_copy(k_hm[D:D + H, slot, odd], diag)
                return last

            dve.wait_ge(const_done, 1)
            head_ones(2)
            head_ones(3).then_inc(ones_done, 1)

            def stacked(dst, n):
                dve.wait_ge(setup_mm, n + 1)
                V.tensor_copy(dst[:], bank[6 + n % 2][:]).then_inc(weights_ready, 1)
                dve.wait_ge(weights_ready, 1 + n // 2)
                V.tensor_tensor(dst[D:P, :], bank[6 + n % 2][D:P, :], dst[D:P, :], ALU.subtract).then_inc(setup_ev, 1)

            stacked(a_w, 0)
            dve.wait_ge(setup_mm, 2)
            V.tensor_copy(woutT[:], bank[7][0:D, :]).then_inc(setup_ev, 1)
            def scale_weights():
                dve.wait_ge(ld_f, 12 * 16)
                for col in (gs_col[:, 0:FT], us_col[:, 0:FT], ts_col[:], ds_col[:]):
                    last = V.tensor_scalar(col, col, SC, None, ALU.mult)
                last.then_inc(scaled, 1)
                dve.wait_ge(scaled, 1)
                for k in range(FT):
                    V.tensor_scalar(gate_raw[:, k, :], gate_raw[:, k, :], gs_col[:, k:k + 1], None, ALU.mult)
                    V.tensor_scalar(up_raw[:, k, :], up_raw[:, k, :], us_col[:, k:k + 1], None, ALU.mult)
                V.tensor_scalar(tail_raw, tail_raw, ts_col[:], None, ALU.mult)
                for k in range(2):
                    last = V.tensor_scalar(down_raw[:, k, :], down_raw[:, k, :], ds_col[:, k:k + 1], None, ALU.mult)
                last.then_inc(scaled, 1)

            def ffn_lo(n, r):
                dve.wait_ge(ffn_set[n], 2)
                src, hi, lo = group_views(n, r)
                V.tensor_tensor(lo, src, hi, ALU.subtract).then_inc(ffn_set[n], 1)

            def max_reduce(e, k):
                it, hp, odd = k // 4, k % 4 // 2, k % 2
                dve.wait_ge(done["mx"], count("mx", e, k))
                if k == first("max", e):
                    wait(dve, done["mt"], count("mt", e.back(2)))
                V.tensor_reduce(nmax[:, e.off % 2, it, 4 * hp + odd:4 * hp + 4:2],
                                in_bank("mx", e, k)[:].rearrange("p (h n) -> p h n", h=2), AX_X, ALU.max,
                                negate=True).then_inc(done["max"], 1)

            def weighted(e, k):
                return in_bank("av", e, k)[:, 0:HG * GW].rearrange("p (h d) -> p h d", h=HG)

            def row_sums(e, k):
                dve.wait_ge(done["av"], count("av", e, k))
                V.reciprocal(rsum[:, e.off % 2, k], weighted(e, k)[:, :, D:GW]).then_inc(done["rsum"], 1)

            def normalise(e, k):
                hg, it = k // 2, k % 2
                dve.wait_ge(done["rsum"], count("rsum", e, k))
                if k == first("norm", e):
                    wait(dve, done["sum"], count("sum", e.back(2), 2))
                V.tensor_tensor(heads[:, e.off % 2, hg * HG:(hg + 1) * HG, it, :], weighted(e, k)[:, :, 0:D],
                                rsum[:, e.off % 2, k].to_broadcast([P, HG, D]), ALU.mult).then_inc(done["norm"], 1)

            def k_rest(e, k):
                dve.wait_ge(done["k_hi"], count("k_hi", e, k))
                wait(dve, mv_k[(e.off - 2) % 4], e.back(2).landed(4, K_MOVES))
                V.tensor_tensor(kk_lo[:, e.off % 2, 2 * k:2 * k + 2, :],
                                in_bank("k", e, k)[:].rearrange("p (j n) -> p j n", j=2),
                                kk_hi[:, e.off % 4, 2 * k:2 * k + 2, :], ALU.subtract).then_inc(done["k_lo"], 1)

            def g_rest(e, jt):
                slot = e.off % 4
                dve.wait_ge(done["g_hi"], count("g_hi", e, jt))
                V.tensor_tensor(g_lo[:, slot, jt, :, :], in_bank("g", e, jt)[:].rearrange("p (h d) -> p h d", h=H),
                                g_hi[:, slot, jt, :, 0:D], ALU.subtract).then_inc(done["g_lo"], 1)

            def ln_stats(e, k):
                dve.wait_ge(ld_x[e.off % 4], e.landed(4, 32))
                V.bn_stats(stats[:, e.off % 2, :], x_in[:, e.off % 4, :]).then_inc(done["stats"], 1)

            def ln_mean(e, k):
                V.bn_aggr(mv[:, e.off % 2, :], stats[:, e.off % 2, :]).then_inc(done["mean"], 1)

            def ln_eps(e, k):
                dve.wait_ge(done["mean"], count("mean", e))
                V.tensor_scalar(var[:, e.off % 2, :], mv[:, e.off % 2, 1:2], EPS, None, ALU.add).then_inc(done["eps"], 1)

            def ln_apply(e, k):
                dve.wait_ge(done["rstd"], count("rstd", e))
                wait(dve, done["x_lo"], count("x_lo", e.back(2)))
                V.tensor_scalar(xn[:, e.off % 2, :], x_in[:, e.off % 4, :], mv[:, e.off % 2, 0:1], rstd[:, e.off % 2, :],
                                ALU.subtract, ALU.mult).then_inc(done["xn"], 1)

            def residual(pr, k):
                slot = pr.off % 2
                dve.wait_ge(done["yt"], count("yt", pr))
                dve.wait_ge(ld_p[slot], pr.landed(2, 16))
                wait(dve, done["finish"], count("finish", pr.back(2)))
                V.scalar_tensor_tensor(out=x2[:, slot, :], in0=in_bank("yt", pr)[:, 0:N], scalar=bout_col[:],
                                       in1=x_pair[:, slot, :], op0=ALU.add, op1=ALU.add).then_inc(done["x2"], 1)

            def ln2_stats(pr, k):
                dve.wait_ge(done["x2"], count("x2", pr))
                V.bn_stats(stats2[:], x2[:, pr.off % 2, :]).then_inc(done["stats2"], 1)

            def ln2_mean(pr, k):
                V.bn_aggr(mv2[:], stats2[:]).then_inc(done["mean2"], 1)

            def ln2_eps(pr, k):
                dve.wait_ge(done["mean2"], count("mean2", pr))
                V.tensor_scalar(var2[:], mv2[:, 1:2], EPS, None, ALU.add).then_inc(done["eps2"], 1)

            def ln2_apply(pr, k):
                dve.wait_ge(done["rstd2"], count("rstd2", pr))
                wait(dve, done["xt"], count("xt", pr.back(1)))
                V.tensor_scalar(xn2[:], x2[:, pr.off % 2, :], mv2[:, 0:1], rstd2[:], ALU.subtract,
                                ALU.mult).then_inc(done["xn2"], 1)

            def xt_rest(pr, k):
                dve.wait_ge(done["xt_hi"], count("xt_hi", pr))
                V.tensor_tensor(xt_lo[:].rearrange("p k n -> p (k n)"), in_bank("xt", pr)[:, 0:N],
                                xt_hi[:].rearrange("p k n -> p (k n)"), ALU.subtract).then_inc(done["xt_lo"], 1)

            def silu_gate(pr, r):
                dve.wait_ge(done["tanh"], count("tanh", pr, r))
                flat = lambda v: v[:, r].rearrange("p k n -> p (k n)")
                V.scalar_tensor_tensor(out=flat(tg), in0=flat(th), scalar=1.0, in1=in_bank("gu", pr, r)[:, 0:2 * P],
                                       op0=ALU.add, op1=ALU.mult).then_inc(done["gate"], 1)

            def times_up(pr, r):
                b, k = in_bank("gu", pr, r), 0.5 / (SC * SC)
                dve.wait_ge(done["gate"], count("gate", pr, r))
                wait(dve, done["h_lo"], count("h_lo", pr.back(1), r))
                if r < 2:
                    last = V.scalar_tensor_tensor(out=h_f[:, r].rearrange("p k n -> p (k n)"),
                                                  in0=tg[:, r].rearrange("p k n -> p (k n)"), scalar=k,
                                                  in1=b[:, 2 * P:4 * P], op0=ALU.mult, op1=ALU.mult)
                else:
                    V.scalar_tensor_tensor(out=h_f[:, 2, 0, :], in0=tg[:, 2, 0, :], scalar=k, in1=b[:, 2 * P:3 * P],
                                           op0=ALU.mult, op1=ALU.mult)
                    last = V.scalar_tensor_tensor(out=h_f[0:TAIL, 2, 1, :], in0=tg[0:TAIL, 2, 1, :], scalar=k,
                                                  in1=b[TAIL:P, P:2 * P], op0=ALU.mult, op1=ALU.mult)
                last.then_inc(done["up"], 1)

            def h_rest(pr, r):
                dve.wait_ge(done["h_hi"], count("h_hi", pr, r))
                if r < 2:
                    last = V.tensor_tensor(h_lo[:, 2 * r:2 * r + 2, :], h_f[:, r], h_hi[:, 2 * r:2 * r + 2, :],
                                           ALU.subtract)
                else:
                    V.tensor_tensor(h_lo[:, 4, :], h_f[:, 2, 0, :], h_hi[:, 4, :], ALU.subtract)
                    last = V.tensor_tensor(h_lo[0:TAIL, 5, :], h_f[0:TAIL, 2, 1, :], h_hi[0:TAIL, 5, :], ALU.subtract)
                last.then_inc(done["h_lo"], 1)

            def finish(pr, k):
                slot = pr.off % 2
                dve.wait_ge(done["down"], count("down", pr))
                wait(dve, st_y[slot], pr.back(2).landed(2, 16))
                V.scalar_tensor_tensor(out=y_out[:, slot, :], in0=in_bank("down", pr)[:, 0:N], scalar=1.0 / SC,
                                       in1=x2[:, slot, :], op0=ALU.mult, op1=ALU.add).then_inc(done["finish"], 1)

            does = {"max": max_reduce, "rsum": row_sums, "norm": normalise, "k_lo": k_rest, "h_lo": h_rest,
                    "g_lo": g_rest, "stats": ln_stats, "mean": ln_mean, "eps": ln_eps, "xn": ln_apply, "x2": residual,
                    "stats2": ln2_stats, "mean2": ln2_mean, "eps2": ln2_eps, "xn2": ln2_apply, "xt_lo": xt_rest,
                    "gate": silu_gate, "up": times_up, "finish": finish}

            STATS_OF = {"mean": "stats", "mean2": "stats2"}

            def step(g, t):
                for position, item in enumerate(DVE_ORDER):
                    nxt = DVE_ORDER[position + 1] if position + 1 < len(DVE_ORDER) else ("", 0, "", 0, -1)
                    if nxt[0] in STATS_OF:
                        assert item[0] != STATS_OF[nxt[0]]
                        e = work(g, t, nxt)
                        if e.live():
                            dve.wait_ge(done[STATS_OF[nxt[0]]], count(STATS_OF[nxt[0]], e))
                    if isinstance(g, int) and (2 * g + t, position) == B_SPLIT_AT:
                        stacked(b_w, 2)
                    if isinstance(g, int) and (2 * g + t, position) == SCALE_WEIGHTS_AT:
                        scale_weights()
                    e = work(g, t, item)
                    if item[0] == "up" and weights_group(e, item[1]) is not None:
                        ffn_lo(weights_group(e, item[1]), item[1])
                    if e.live():
                        does[item[0]](e, item[1])

            walk(dve, step)

        @block.gpsimd
        def _(pool):
            G = nc.gpsimd
            G.memset(ident[:], 0.0).then_inc(memset_done, 1)
            pool.wait_ge(memset_done, 1)
            G.affine_select(out=ident[:], in_=ident[:], compare_op=ALU.not_equal, fill=1.0, base=0,
                            pattern=[[-1, P]], channel_multiplier=1).then_inc(const_done, 1)
            G.memset(g_hi[:, :, :, :, D:GW], 1.0)
            G.memset(neg_half[:], -0.5).then_inc(memset_done, 1)
            pool.wait_ge(memset_done, 2)

            def p_rest(e, u):
                pool.wait_ge(done["p_hi"], count("p_hi", e, u))
                row = lambda v: v.rearrange("p h n -> p (h n)")
                G.tensor_tensor(row(p_lo[:, e.off % 2, u]), row(p_f[:, e.off % 2, u]), row(p_hi[:, e.off % 2, u]),
                                ALU.subtract).then_inc(done["p_lo"], 1)

            def head_sum(e, part):
                if part == 0:
                    pool.wait_ge(done["norm"], count("norm", e, final("norm", e, range(4))))
                    o, a, b = heads[:, e.off % 2, 0:4], heads[:, e.off % 2, 0:4], heads[:, e.off % 2, 4:8]
                elif part == 1:
                    pool.wait_ge(done["sum"], count("sum", e, 0))
                    o, a, b = heads[:, e.off % 2, 0:2], heads[:, e.off % 2, 0:2], heads[:, e.off % 2, 2:4]
                else:
                    pool.wait_ge(done["sum"], count("sum", e, 1))
                    wait(pool, done["yt"], count("yt", At(e.g, 2, e.off // 2 - 2, NPAIR)))
                    if isinstance(e.g, int) and 4 * e.g + e.off < 2:
                        for n in range(3):
                            pool.wait_ge(ffn_set[n], 1)
                    o, a, b = yT[:, e.off // 2 % 2, :, e.off % 2, :], heads[:, e.off % 2, 0], heads[:, e.off % 2, 1]
                G.tensor_tensor(o, a, b, ALU.add).then_inc(done["sum"], 1)

            def x_rest(e, k):
                pool.wait_ge(done["x_hi"], count("x_hi", e))
                G.tensor_tensor(x_lom[0:D, e.off % 4, :], xn[0:D, e.off % 2, :], x_hi[0:D, e.off % 4, :],
                                ALU.subtract).then_inc(done["x_lo"], 1)

            def c_rest(e, k):
                pool.wait_ge(done["c_hi"], count("c_hi", e))
                G.tensor_tensor(c_lo[:, e.off % 2, :], c_in[:, e.off % 4, :], c_hi[:, e.off % 2, :],
                                ALU.subtract).then_inc(done["c_lo"], 1)

            def ln_rstd(e, k):
                pool.wait_ge(done["eps"], count("eps", e))
                G.tensor_tensor(rstd[:, e.off % 2, :], var[:, e.off % 2, :], neg_half[:],
                                ALU.pow).then_inc(done["rstd"], 1)

            def ln2_rstd(pr, k):
                pool.wait_ge(done["eps2"], count("eps2", pr))
                G.tensor_tensor(rstd2[:], var2[:], neg_half[:], ALU.pow).then_inc(done["rstd2"], 1)

            does = {"p_lo": p_rest, "sum": head_sum, "x_lo": x_rest, "c_lo": c_rest, "rstd": ln_rstd,
                    "rstd2": ln2_rstd}

            def step(g, t):
                for item in POOL_ORDER:
                    e = work(g, t, item)
                    if e.live():
                        does[item[0]](e, item[1])

            walk(pool, step)


_INS = ["x", "ctx_2048", "L0_xattn_Wq", "L0_xattn_Wkv", "L0_xattn_Wout", "L0_xattn_bout", "L0_ffn_gate_w",
        "L0_ffn_up_w", "L0_ffn_down_w", "L0_ffn_gate_s", "L0_ffn_up_s", "L0_ffn_down_s"]


def kernel(**inputs):
    import numpy as _np
    import concourse.bacc as _bacc
    from concourse import mybir as _mybir
    from concourse.bass_utils import run_bass_kernel_spmd as _run

    nc = _bacc.Bacc("TRN2", target_bir_lowering=False, num_devices=1)
    arrays, args = {}, []
    for name in _INS:
        a = _np.ascontiguousarray(inputs[name])
        arrays[f"in_{name}_dram"] = a
        args.append(nc.dram_tensor(f"in_{name}_dram", a.shape, _mybir.dt.from_np(a.dtype), kind="ExternalInput").ap())
    dt = _mybir.dt.from_np(_np.dtype("float32"))
    args.append(nc.dram_tensor("out_dram", inputs["x"].shape, dt, kind="ExternalOutput").ap())
    xattn_ffn(nc, *args)
    r = _run(nc, [arrays], core_ids=[0])
    return r.results[0]["out_dram"]
```
